# Optimizing a Trainium2 kernel written in Bass

```python
import numpy as np
import jax
import jax.numpy as jnp

def _softmax(x, axis=-1):
    return jax.nn.softmax(x, axis=axis)

def _gelu(x):
    return jax.nn.gelu(x, approximate=True)

def _silu(x):
    return jax.nn.silu(x)

def _sigmoid(x):
    return jax.nn.sigmoid(x)

def _layernorm(x, axis=-1, eps=1e-05):
    m = jnp.mean(x, axis=axis, keepdims=True)
    v = jnp.var(x, axis=axis, keepdims=True)
    return (x - m) / jnp.sqrt(v + eps)

def _scatter_add(tgt, idx, src, axis=0):
    return tgt.at[idx].add(src)

def _segment_sum(src, seg, n):
    return jax.ops.segment_sum(src, seg, n)
kernel_name = 'mk_hybrid_d1_jaxref_r8_7f718a'

def setup_inputs(seed: int=0):
    np.random.seed(seed)
    _w = jnp.asarray

    def _L0_attn_a_setup():
        import jax, jax.numpy as jnp
        import numpy as np
        B, S, E, H, D = (4, 256, 128, 16, 64)

        def _large_negative_number(dtype):
            return jnp.asarray(-0.7 * jnp.finfo(dtype).max, dtype=dtype)
        key = jax.random.key(seed)
        k1, k2, k3 = jax.random.split(key, 3)
        x = jax.random.normal(k1, (B, S, E), dtype=jnp.float32)
        qkv_w = jax.random.normal(k2, (E, H, 3 * D), dtype=jnp.float32) * (1.0 / np.sqrt(E))
        qkv_b = jnp.zeros((H, 3 * D), dtype=jnp.float32)
        out_w = jax.random.normal(k3, (H, D, E), dtype=jnp.float32) * (1.0 / np.sqrt(H * D))
        out_b = jnp.zeros((E,), dtype=jnp.float32)
        return {'x': x, 'qkv_w': qkv_w, 'qkv_b': qkv_b, 'out_w': out_w, 'out_b': out_b}
    _L0_attn_a_in = _L0_attn_a_setup()

    def _L0_attn_b_setup():
        import jax, jax.numpy as jnp
        import numpy as np
        D_MODEL = 128
        D_STATE = 128
        D_CONV = 4
        EXPAND = 2
        HEADDIM = 64
        D_INNER = EXPAND * D_MODEL
        NHEADS = D_INNER // HEADDIM
        D_IN_PROJ = 2 * D_INNER + 2 * D_STATE + NHEADS
        CONV_DIM = D_INNER + 2 * D_STATE

        def _block_norm(x, w, eps=1e-06):
            return w * x / jnp.sqrt(jnp.sum(x * x, axis=-1, keepdims=True) + eps)

        def _mamba2(x, in_proj_w, conv_w, conv_b, dt_bias, A_log, D, mnorm_w, out_proj_w):
            b, l, _ = x.shape
            zxbcdt = x @ in_proj_w.T
            z, xBC, dt_raw = jnp.split(zxbcdt, [D_INNER, D_INNER + CONV_DIM], axis=-1)
            pad = jnp.pad(xBC, ((0, 0), (D_CONV - 1, 0), (0, 0)))
            conv = sum((pad[:, k:k + l, :] * conv_w[None, None, :, k] for k in range(D_CONV))) + conv_b
            xBC = jax.nn.silu(conv)
            xh, Bm, Cm = jnp.split(xBC, [D_INNER, D_INNER + D_STATE], axis=-1)
            xh = xh.reshape(b, l, NHEADS, HEADDIM)
            dt = jax.nn.softplus(dt_raw + dt_bias)
            A = -jnp.exp(A_log)

            def step(hs, inp):
                x_t, dt_t, B_t, C_t = inp
                dA = jnp.exp(dt_t * A)[:, :, None, None]
                hs = hs * dA + (dt_t[:, :, None] * x_t)[..., None] * B_t[:, None, None, :]
                y_t = jnp.einsum('bhpn,bn->bhp', hs, C_t)
                return (hs, y_t)
            hs0 = jnp.zeros((b, NHEADS, HEADDIM, D_STATE), x.dtype)
            _, ys = jax.lax.scan(step, hs0, (xh.transpose(1, 0, 2, 3), dt.transpose(1, 0, 2), Bm.transpose(1, 0, 2), Cm.transpose(1, 0, 2)))
            y = ys.transpose(1, 0, 2, 3) + D[None, None, :, None] * xh
            y = y.reshape(b, l, D_INNER)
            y = y * jax.nn.silu(z)
            y = y / jnp.sqrt(jnp.mean(y * y, axis=-1, keepdims=True) + 1e-05) * mnorm_w
            return y @ out_proj_w.T
        key = jax.random.key(seed)
        ks = jax.random.split(key, 8)
        B, L = (2, 256)
        s = lambda k, shape, sc=0.02: jax.random.normal(k, shape, jnp.float32) * sc
        return dict(x=jax.random.normal(ks[0], (B, L, D_MODEL), jnp.float32), norm1_w=jnp.ones((D_MODEL,), jnp.float32), in_proj_w=s(ks[1], (D_IN_PROJ, D_MODEL)), conv_w=s(ks[2], (CONV_DIM, D_CONV), 0.2), conv_b=jnp.zeros((CONV_DIM,), jnp.float32), dt_bias=jnp.log(jnp.expm1(jax.random.uniform(ks[3], (NHEADS,), jnp.float32, 0.001, 0.1))), A_log=jnp.log(jax.random.uniform(ks[4], (NHEADS,), jnp.float32, 1.0, 16.0)), D=jnp.ones((NHEADS,), jnp.float32), mnorm_w=jnp.ones((D_INNER,), jnp.float32), out_proj_w=s(ks[5], (D_MODEL, D_INNER)), norm2_w=jnp.ones((D_MODEL,), jnp.float32), mlp_w1=s(ks[6], (4 * D_MODEL, D_MODEL)), mlp_b1=jnp.zeros((4 * D_MODEL,), jnp.float32), mlp_w2=s(ks[7], (D_MODEL, 4 * D_MODEL)), mlp_b2=jnp.zeros((D_MODEL,), jnp.float32))
    _L0_attn_b_in = _L0_attn_b_setup()

    def _L0_ffn_setup():
        import jax, jax.numpy as jnp
        import numpy as np
        ALPHA = 1.0
        key = jax.random.key(seed)
        ks = jax.random.split(key, 7)
        B, S, IN, OUT = (8, 1024, 128, 128)
        RANK, DDIM, UDIM = (4, 100, 50)
        return {'hidden_states': jax.random.normal(ks[0], (B, S, IN), dtype=jnp.float32), 'W': jax.random.normal(ks[1], (OUT, IN), dtype=jnp.float32) * 0.02, 'b': jax.random.normal(ks[2], (OUT,), dtype=jnp.float32) * 0.02, 'lora_down': jax.random.normal(ks[3], (RANK, DDIM), dtype=jnp.float32) * 0.1, 'lora_up': jax.random.normal(ks[4], (UDIM, RANK), dtype=jnp.float32) * 0.1, 'down_aux': jax.random.normal(ks[5], (DDIM, IN), dtype=jnp.float32) * 0.03, 'up_aux': jax.random.normal(ks[6], (OUT, UDIM), dtype=jnp.float32) * 0.03}
    _L0_ffn_in = _L0_ffn_setup()
    _d = {'L0_attn_a_x': _L0_attn_a_in['x'], 'L0_attn_a_qkv_w': _L0_attn_a_in['qkv_w'], 'L0_attn_a_qkv_b': _L0_attn_a_in['qkv_b'], 'L0_attn_a_out_w': _L0_attn_a_in['out_w'], 'L0_attn_a_out_b': _L0_attn_a_in['out_b'], 'L0_attn_b_norm1_w': _L0_attn_b_in['norm1_w'], 'L0_attn_b_in_proj_w': _L0_attn_b_in['in_proj_w'], 'L0_attn_b_conv_w': _L0_attn_b_in['conv_w'], 'L0_attn_b_conv_b': _L0_attn_b_in['conv_b'], 'L0_attn_b_dt_bias': _L0_attn_b_in['dt_bias'], 'L0_attn_b_A_log': _L0_attn_b_in['A_log'], 'L0_attn_b_D': _L0_attn_b_in['D'], 'L0_attn_b_mnorm_w': _L0_attn_b_in['mnorm_w'], 'L0_attn_b_out_proj_w': _L0_attn_b_in['out_proj_w'], 'L0_attn_b_norm2_w': _L0_attn_b_in['norm2_w'], 'L0_attn_b_mlp_w1': _L0_attn_b_in['mlp_w1'], 'L0_attn_b_mlp_b1': _L0_attn_b_in['mlp_b1'], 'L0_attn_b_mlp_w2': _L0_attn_b_in['mlp_w2'], 'L0_attn_b_mlp_b2': _L0_attn_b_in['mlp_b2'], 'L0_ffn_W': _L0_ffn_in['W'], 'L0_ffn_b': _L0_ffn_in['b'], 'L0_ffn_lora_down': _L0_ffn_in['lora_down'], 'L0_ffn_lora_up': _L0_ffn_in['lora_up'], 'L0_ffn_down_aux': _L0_ffn_in['down_aux'], 'L0_ffn_up_aux': _L0_ffn_in['up_aux']}
    _x0 = _d['L0_attn_a_x']
    _d['L0_attn_a_x'] = jax.random.normal(jax.random.fold_in(jax.random.key(seed), 1), (8, 512, 128), dtype=_x0.dtype)
    del _x0
    return _d

def reference(L0_attn_a_x, L0_attn_a_qkv_w, L0_attn_a_qkv_b, L0_attn_a_out_w, L0_attn_a_out_b, L0_attn_b_norm1_w, L0_attn_b_in_proj_w, L0_attn_b_conv_w, L0_attn_b_conv_b, L0_attn_b_dt_bias, L0_attn_b_A_log, L0_attn_b_D, L0_attn_b_mnorm_w, L0_attn_b_out_proj_w, L0_attn_b_norm2_w, L0_attn_b_mlp_w1, L0_attn_b_mlp_b1, L0_attn_b_mlp_w2, L0_attn_b_mlp_b2, L0_ffn_W, L0_ffn_b, L0_ffn_lora_down, L0_ffn_lora_up, L0_ffn_down_aux, L0_ffn_up_aux):

    def _L0_attn_a_ref(x, qkv_w, qkv_b, out_w, out_b):
        import jax, jax.numpy as jnp
        import numpy as np
        B, S, E, H, D = (4, 256, 128, 16, 64)

        def _large_negative_number(dtype):
            return jnp.asarray(-0.7 * jnp.finfo(dtype).max, dtype=dtype)
        qkv = jnp.einsum('bse,ehd->bshd', x, qkv_w) + qkv_b
        q, k, v = jnp.split(qkv, 3, axis=-1)
        logits = jnp.einsum('bqhd,bkhd->bhqk', q, k)
        logits = logits / jnp.sqrt(jnp.asarray(q.shape[-1], logits.dtype))
        mask = jnp.tril(jnp.ones((q.shape[1], q.shape[1]), dtype=jnp.bool_))
        logits = jnp.where(mask, logits, _large_negative_number(logits.dtype))
        probs = jax.nn.softmax(logits, axis=-1)
        attn = jnp.einsum('bhqk,bkhd->bqhd', probs, v)
        return jnp.einsum('bqhd,hde->bqe', attn, out_w) + out_b

    def _L0_attn_b_ref(x, norm1_w, in_proj_w, conv_w, conv_b, dt_bias, A_log, D, mnorm_w, out_proj_w, norm2_w, mlp_w1, mlp_b1, mlp_w2, mlp_b2):
        import jax, jax.numpy as jnp
        import numpy as np
        D_MODEL = 128
        D_STATE = 128
        D_CONV = 4
        EXPAND = 2
        HEADDIM = 64
        D_INNER = EXPAND * D_MODEL
        NHEADS = D_INNER // HEADDIM
        D_IN_PROJ = 2 * D_INNER + 2 * D_STATE + NHEADS
        CONV_DIM = D_INNER + 2 * D_STATE

        def _block_norm(x, w, eps=1e-06):
            return w * x / jnp.sqrt(jnp.sum(x * x, axis=-1, keepdims=True) + eps)

        def _mamba2(x, in_proj_w, conv_w, conv_b, dt_bias, A_log, D, mnorm_w, out_proj_w):
            b, l, _ = x.shape
            zxbcdt = x @ in_proj_w.T
            z, xBC, dt_raw = jnp.split(zxbcdt, [D_INNER, D_INNER + CONV_DIM], axis=-1)
            pad = jnp.pad(xBC, ((0, 0), (D_CONV - 1, 0), (0, 0)))
            conv = sum((pad[:, k:k + l, :] * conv_w[None, None, :, k] for k in range(D_CONV))) + conv_b
            xBC = jax.nn.silu(conv)
            xh, Bm, Cm = jnp.split(xBC, [D_INNER, D_INNER + D_STATE], axis=-1)
            xh = xh.reshape(b, l, NHEADS, HEADDIM)
            dt = jax.nn.softplus(dt_raw + dt_bias)
            A = -jnp.exp(A_log)

            def step(hs, inp):
                x_t, dt_t, B_t, C_t = inp
                dA = jnp.exp(dt_t * A)[:, :, None, None]
                hs = hs * dA + (dt_t[:, :, None] * x_t)[..., None] * B_t[:, None, None, :]
                y_t = jnp.einsum('bhpn,bn->bhp', hs, C_t)
                return (hs, y_t)
            hs0 = jnp.zeros((b, NHEADS, HEADDIM, D_STATE), x.dtype)
            _, ys = jax.lax.scan(step, hs0, (xh.transpose(1, 0, 2, 3), dt.transpose(1, 0, 2), Bm.transpose(1, 0, 2), Cm.transpose(1, 0, 2)))
            y = ys.transpose(1, 0, 2, 3) + D[None, None, :, None] * xh
            y = y.reshape(b, l, D_INNER)
            y = y * jax.nn.silu(z)
            y = y / jnp.sqrt(jnp.mean(y * y, axis=-1, keepdims=True) + 1e-05) * mnorm_w
            return y @ out_proj_w.T
        x = x + _mamba2(_block_norm(x, norm1_w), in_proj_w, conv_w, conv_b, dt_bias, A_log, D, mnorm_w, out_proj_w)
        h = _block_norm(x, norm2_w)
        h = jax.nn.gelu(h @ mlp_w1.T + mlp_b1, approximate=False) @ mlp_w2.T + mlp_b2
        return x + h

    def _L0_ffn_ref(hidden_states, W, b, lora_down, lora_up, down_aux, up_aux):
        import jax, jax.numpy as jnp
        import numpy as np
        ALPHA = 1.0
        lilora_weight = up_aux @ (lora_up @ (lora_down @ down_aux))
        base = jnp.einsum('bsi,oi->bso', hidden_states, W) + b
        delta = jnp.einsum('bsi,oi->bso', hidden_states, lilora_weight)
        return base + ALPHA * delta
    x = L0_attn_a_x
    x = x + _L0_attn_a_ref(_layernorm(x, axis=-1), L0_attn_a_qkv_w, L0_attn_a_qkv_b, L0_attn_a_out_w, L0_attn_a_out_b)
    x = x + _L0_ffn_ref(_layernorm(x, axis=-1), L0_ffn_W, L0_ffn_b, L0_ffn_lora_down, L0_ffn_lora_up, L0_ffn_down_aux, L0_ffn_up_aux)
    x = x + _L0_attn_b_ref(_layernorm(x, axis=-1), L0_attn_b_norm1_w, L0_attn_b_in_proj_w, L0_attn_b_conv_w, L0_attn_b_conv_b, L0_attn_b_dt_bias, L0_attn_b_A_log, L0_attn_b_D, L0_attn_b_mnorm_w, L0_attn_b_out_proj_w, L0_attn_b_norm2_w, L0_attn_b_mlp_w1, L0_attn_b_mlp_b1, L0_attn_b_mlp_w2, L0_attn_b_mlp_b2)
    x = x + _L0_ffn_ref(_layernorm(x, axis=-1), L0_ffn_W, L0_ffn_b, L0_ffn_lora_down, L0_ffn_lora_up, L0_ffn_down_aux, L0_ffn_up_aux)
    return x

_drawn_inputs = setup_inputs


def setup_inputs(seed=0):
    import zlib

    import numpy as np

    out = dict(_drawn_inputs(seed))
    spreads = {'L0_attn_a_qkv_b': (0.0, 0.1),
     'L0_attn_a_out_b': (0.0, 0.1),
     'L0_attn_b_norm1_w': (1.0, 0.6),
     'L0_attn_b_conv_b': (0.0, 0.296),
     'L0_attn_b_D': (1.0, 0.6),
     'L0_attn_b_mnorm_w': (1.0, 0.6),
     'L0_attn_b_norm2_w': (1.0, 0.6),
     'L0_attn_b_mlp_b1': (0.0, 0.8),
     'L0_attn_b_mlp_b2': (0.0, 0.1)}
    factors = {'L0_attn_b_conv_w': 8.0,
     'L0_attn_b_dt_bias': 8.0,
     'L0_attn_b_A_log': 8.0,
     'L0_attn_b_mlp_w1': 8.0,
     'L0_attn_b_mlp_w2': 5.714,
     'L0_ffn_lora_down': 2.754,
     'L0_ffn_lora_up': 3.044,
     'L0_ffn_up_aux': 2.821}
    for name, (base, spread) in spreads.items():
        noise = np.random.default_rng([zlib.crc32(name.encode()), seed]).standard_normal(out[name].shape)
        drawn = base * np.exp(spread * noise) if base else spread * noise
        out[name] = jnp.asarray(drawn.astype(out[name].dtype))
    for name, factor in factors.items():
        out[name] = (out[name] * factor).astype(out[name].dtype)
    return out
```

```python
from contextlib import ExitStack

import numpy as np

import concourse.bass as bass
from concourse import mybir

F32 = mybir.dt.float32
F32R = mybir.dt.float32r
ALU = mybir.AluOpType
ACT = mybir.ActivationFunctionType

P = 128
TOK = 512
NT = TOK // P
HEADS = 16
HD = 64
PAIRS = HEADS // 2
TRI = NT * (NT + 1) // 2 * P
MHEADS = 4
INNER = 256
CONV = 4
LN_EPS = 1e-5
BN_EPS = 1e-6
SCALE = HD ** -0.5
MASKED = -0.7 * float(np.finfo(np.float32).max)
LOG_TERMS = 8

TRI_AT = [P * t * (t + 1) // 2 for t in range(NT)]
BC_TILES = ((0,), (1, 3), (2,))
COL_AT = [P * (NT * j - j * (j - 1) // 2) for j in range(NT)]

NAMES = """
x_loaded x_mv x_rstd xb_ready xn_ready xnT_full hT_ready hTh_ready hTl_ready
v_full v_evac_act v_evac_dve
g_full g_evac gh_ready gl_ready s_full sm_ready p_ready t_full pt_act pt_dve
rden_ready spread_ready pv_done o_ready y_full x1_ready
misc_full0 misc_full1 misc_free0 misc_free1
dve_chain pool_chain
a_mv a_rstd n1_ready x1b_ready
b_mv b_r12 n_ready
dt_abs dt_exp dt_ready dta_ready da_ready
conv_ready silu_ready m_ready
yz_ready y2_ready rs_ready ss2_ready r3_ready h3_ready x2b_ready
d_mv d_rstd n4_ready x3b_ready
out_dma
""".split()


def tile_cols(t):
    return P * (t + 1)


def layer(nc, a, out):
    with ExitStack() as ctx:
        def sb(name, shape, dt=F32):
            return ctx.enter_context(nc.sbuf_tensor(name, shape, dt))

        def bank(name):
            return ctx.enter_context(nc.psum_tensor(name, [P, 512], F32))

        psS = [bank("psS0"), bank("psS1")]
        psT = [bank("psT0"), bank("psT1")]
        psG = bank("psG")
        psO = bank("psO")
        psX = [bank("psX0"), bank("psX1")]

        mask = sb("mask", [P, TOK])
        eye_row = sb("eye_row", [P, TOK])
        ident = eye_row[:, 0:P]
        ones = sb("ones", [P, 1])
        neg_half = sb("neg_half", [P, NT])
        neg_one = sb("neg_one", [P, NT * MHEADS])
        PT = [sb(f"PT{i}", [P, NT, TOK]) for i in range(4)]
        wq_t = PT[0][:, 0:2, :].rearrange("p a (b e) -> p (a b) e", e=P)
        wk_t = PT[0][:, 2:4, :].rearrange("p a (b e) -> p (a b) e", e=P)
        wv = PT[1][:, 0:2, :].rearrange("p a c -> p (a c)")
        wo = sb("wo", [P, PAIRS, P])
        bq = sb("bq", [P, PAIRS])
        bv = sb("bv", [P, PAIRS])
        row_out_b = sb("row_out_b", [P, P])
        ffn_wt = sb("ffn_wt", [P, P])
        ffn_b = sb("ffn_b", [P, P])
        up_t = sb("up_t", [50, P])
        lora_up_t = sb("lora_up_t", [4, 50])
        lora_down_t = sb("lora_down_t", [100, 4])
        down_aux = sb("down_aux", [100, P])
        norm1 = sb("norm1", [P, 1])
        norm2 = sb("norm2", [P, 1])
        win_t = sb("win_t", [P, 772])
        conv_w = sb("conv_w", [P, 4, CONV])
        conv_b = sb("conv_b", [P, 4])
        dt_bias = sb("dt_bias", [P, NT * MHEADS])
        a_log = sb("a_log", [P, NT * MHEADS])
        d_col = sb("d_col", [P, 2])
        mnorm = sb("mnorm", [P, 2])
        wmo = sb("wmo", [P, 2, P])
        w1 = sb("w1", [P, 4 * P])
        b1 = sb("b1", [P, 4])
        w2 = sb("w2", [P, 4, P])
        b2 = sb("b2", [P, P])
        lora1 = sb("lora1", [4, P])
        lora2 = sb("lora2", [50, P])
        cq = sb("cq", [P, HEADS])
        mh = sb("mh", [P, HEADS, P], F32R)
        ml = sb("ml", [P, HEADS, P], F32R)
        wvh = sb("wvh", [P, HEADS * HD], F32R)
        wvl = sb("wvl", [P, HEADS * HD], F32R)
        neg_a = sb("neg_a", [P, NT * MHEADS])

        xin = sb("xin", [P, NT, P])
        x_st = sb("x_st", [P, NT, 6])
        x_mv = sb("x_mv", [P, NT, 2])
        x_veps = sb("x_veps", [P, NT])
        x_rstd = sb("x_rstd", [P, NT])
        xn = sb("xn", [P, NT, P])
        hT = sb("hT", [P, TOK])
        hTh = sb("hTh", [P, TOK], F32R)
        hTl = sb("hTl", [P, TOK], F32R)
        V = sb("V", [P, NT, HEADS * HD])
        G = sb("G", [P, TOK])
        Gh = [sb(f"Gh{i}", [P, TOK], F32R) for i in range(2)]
        Gl = [sb(f"Gl{i}", [P, TOK], F32R) for i in range(2)]
        Sm = [sb(f"Sm{i}", [P, TOK]) for i in range(3)]
        nb = sb("nb", [P, HEADS * NT])
        den = sb("den", [P, HEADS, NT])
        rden = sb("rden", [P, HEADS, NT])
        Pr = [sb(f"Pr{i}", [P, TRI]) for i in range(2)]
        R = sb("R", [P, TOK])
        x1 = sb("x1", [P, NT, P])

        st = sb("st", [P, NT, 6])
        a_mv = sb("a_mv", [P, NT, 2])
        a_veps = sb("a_veps", [P, NT])
        a_rstd = sb("a_rstd", [P, NT])
        n1 = sb("n1", [P, NT, P])
        x1b = sb("x1b", [P, NT, P])
        n1T = sb("n1T", [P, TOK])
        x2 = sb("x2", [P, NT, P])
        st2 = sb("st2", [P, NT, 6])
        b_mv = sb("b_mv", [P, NT, 2])
        b_veps = sb("b_veps", [P, NT])
        b_r1 = sb("b_r1", [P, NT])
        b_sq = sb("b_sq", [P, NT])
        b_r2 = sb("b_r2", [P, NT])
        b_r12 = sb("b_r12", [P, NT])
        u = sb("u", [P, NT, P])
        nn = sb("nn", [P, NT, P])
        nT = sb("nT", [P, TOK])
        dtx = sb("dtx", [P, NT * MHEADS])
        dt_abs = sb("dt_absx", [P, NT * MHEADS])
        dt_exp = sb("dt_expx", [P, NT * MHEADS])
        dt_s = sb("dt_s", [P, NT * MHEADS])
        dt_s2 = sb("dt_s2", [P, NT * MHEADS])
        dt_poly = sb("dt_poly", [P, NT * MHEADS])
        dta = sb("dta", [P, NT * MHEADS])
        dt = sb("dt", [P, NT * MHEADS])
        dA = sb("dA", [P, NT * MHEADS])
        pad = sb("pad", [P, 4, CONV - 1 + TOK])
        xbc = sb("xbc", [P, 4, TOK])
        zs = sb("zs", [P, 2, TOK])
        xdt = sb("xdt", [P, NT, INNER])
        bc = sb("bc", [P, TRI])
        Lall = sb("Lall", [P, 2 * TRI])
        L = [Lall[:, i * TRI:(i + 1) * TRI] for i in range(2)]

        def in_l(i):
            return Lall[:, i * TOK:(i + 1) * TOK].rearrange("p (t e) -> p t e", e=P)

        Mall = sb("Mall", [P, 2 * TRI])
        M = [Mall[:, i * TRI:(i + 1) * TRI] for i in range(2)]
        acc = [Mall[:, c * TOK:(c + 1) * TOK] for c in range(4)]
        gl = Mall[:, 0:4 * TOK].rearrange("p (f n) -> p f n", f=4)
        yd = sb("yd", [P, 2, TOK])
        yz = sb("yz", [P, 2, TOK])
        y2 = yd
        ss = sb("ss", [P, NT])
        rs = sb("rs", [P, NT])
        u2 = in_l(0)
        usq = in_l(1)
        ss2 = sb("ss2", [P, NT])
        r3_eps = sb("r3_eps", [P, NT])
        r3 = sb("r3", [P, NT])
        h3 = in_l(2)
        x2b = in_l(3)
        h3T = Lall[:, 4 * TOK:5 * TOK]
        x3 = x1b
        st4 = sb("st4", [P, NT, 6])
        d_mv = sb("d_mv", [P, NT, 2])
        d_veps = sb("d_veps", [P, NT])
        d_rstd = sb("d_rstd", [P, NT])
        n4 = n1
        x3b = nn
        n4T = n1T
        x4 = x2

        s = {n: ctx.enter_context(nc.semaphore(n)) for n in NAMES}
        nums = sorted(q.num for q in s.values())
        assert nums == list(range(nums[0], nums[0] + len(nums)))
        loop_sems = range(nums[0], nums[-1] + 1)
        misc_full = [s["misc_full0"], s["misc_full1"]]
        misc_free = [s["misc_free0"], s["misc_free1"]]

        loaded = ctx.enter_context(nc.semaphore("weights_loaded"))
        su_pe = ctx.enter_context(nc.semaphore("setup_products"))
        su_dve = ctx.enter_context(nc.semaphore("setup_dve"))
        su_act = ctx.enter_context(nc.semaphore("setup_act"))
        su_pool = ctx.enter_context(nc.semaphore("setup_pool"))

        loads_sync = [(wq_t, "wq_t"), (wk_t, "wk_t"), (wv, "wv"), (wo[:], "wo"), (mask[:], "mask"),
                      (win_t[:], "win_t"), (w1[:], "w1"), (w2[:], "w2"), (wmo[:], "wmo")]
        loads_act = [(eye_row, "eye_row"), (bq, "bq"), (bv, "bv"), (row_out_b, "out_b"),
                     (ffn_wt, "ffn_wt"), (ffn_b, "ffn_b"), (up_t, "up_t"), (lora_up_t, "lora_up_t"),
                     (lora_down_t, "lora_down_t"), (down_aux, "down_aux"), (norm1, "norm1"),
                     (norm2, "norm2"), (conv_w, "conv_w"), (conv_b, "conv_b"), (dt_bias, "dt_bias"),
                     (a_log, "a_log"), (d_col, "d_col"), (mnorm, "mnorm"), (b1, "b1"), (b2, "b2")]
        ALL_LOADED = 16 * (len(loads_sync) + len(loads_act))

        with nc.Block() as block:
            @block.sync
            def _(sp):
                for t, name in loads_sync:
                    sp.dma_start(t, a[name]).then_inc(loaded, 16)

            @block.gpsimd
            def _(pool):
                nc.gpsimd.memset(ones[:], 1.0)
                nc.gpsimd.memset(neg_half[:], -0.5)
                nc.gpsimd.memset(neg_one[:], -1.0)
                nc.gpsimd.memset(pad[:], 0.0).then_inc(su_pool, 1)

            @block.tensor
            def _(pe):
                pe.wait_ge(loaded, ALL_LOADED)
                for h in range(HEADS):
                    half = slice(HD * (h % 2), HD * (h % 2) + HD)
                    ps = (psT if h % 2 else psS)[h // 8]
                    at = P * (h % 8 // 2)
                    last = nc.tensor.matmul(ps[:, at:at + P], wq_t[half, h // 2, :],
                                            wk_t[half, h // 2, :], start=True, stop=True)
                last.then_inc(su_pe, 1)
                for h in range(HEADS):
                    half = slice(HD * (h % 2), HD * (h % 2) + HD)
                    last = nc.tensor.matmul((psO if h % 2 else psG)[:, 256 + h:257 + h], wk_t[half, h // 2, :], bq[half, h // 2:h // 2 + 1],
                                            start=True, stop=True)
                last.then_inc(su_pe, 1)
                for p in range(PAIRS):
                    last = nc.tensor.matmul(psO[:, 0:P], bv[:, p:p + 1].to_broadcast([P, P]), wo[:, p, :],
                                            start=(p == 0), stop=(p == PAIRS - 1))
                last.then_inc(su_pe, 1)
                nc.tensor.matmul(psX[0][0:4, 0:P], lora_down_t[:], down_aux[:], start=True, stop=True).then_inc(su_pe, 1)
                pe.wait_ge(su_act, 2)
                nc.tensor.matmul(psX[1][0:50, 0:P], lora_up_t[:], lora1[:], start=True, stop=True).then_inc(su_pe, 1)
                pe.wait_ge(su_act, 3)
                nc.tensor.matmul(psX[0][:, 0:P], lora2[:], up_t[:], start=True, stop=True).then_inc(su_pe, 1)

            @block.scalar
            def _(act):
                for t, name in loads_act:
                    act.dma_start(t[:], a[name]).then_inc(loaded, 16)
                act.wait_ge(loaded, ALL_LOADED)
                nc.scalar.activation(neg_a[:], a_log[:], ACT.Exp).then_inc(su_act, 1)
                act.wait_ge(su_pe, 4)
                nc.scalar.copy(lora1[:], psX[0][0:4, 0:P]).then_inc(su_act, 1)
                act.wait_ge(su_pe, 5)
                nc.scalar.copy(lora2[:], psX[1][0:50, 0:P]).then_inc(su_act, 1)

            @block.vector
            def _(dve):
                dve.wait_ge(loaded, ALL_LOADED)
                nc.vector.tensor_copy(wvh[:], wv).then_inc(su_dve, 1)
                nc.vector.tensor_scalar(win_t[:], win_t[:], norm1[:, 0:1], None, ALU.mult)
                nc.vector.tensor_scalar(w1[:], w1[:], norm2[:, 0:1], None, ALU.mult)
                for k in range(2):
                    nc.vector.tensor_scalar(wmo[:, k, :], wmo[:, k, :], mnorm[:, k:k + 1], None, ALU.mult)
                dve.wait_ge(su_dve, 1)
                nc.vector.tensor_tensor(wvl[:], wv, wvh[:].bitcast(F32), ALU.subtract)
                dve.wait_ge(su_act, 1)
                nc.vector.tensor_scalar(neg_a[:], neg_a[:], -1.0, None, ALU.mult)
                dve.wait_ge(su_pe, 1)
                four = [slice(8 * k + odd, 8 * k + odd + 7, 2) for odd in range(2) for k in range(2)]
                for heads, ps in zip(four, psS + psT):
                    nc.vector.tensor_copy(mh[:, heads, :], ps[:].rearrange("p (h e) -> p h e", e=P)).then_inc(su_dve, 1)
                dve.wait_ge(su_dve, 5)
                for heads, ps in zip(four, psS + psT):
                    nc.vector.tensor_tensor(ml[:, heads, :], ps[:].rearrange("p (h e) -> p h e", e=P),
                                            mh[:, heads, :].bitcast(F32), ALU.subtract)
                dve.wait_ge(su_pe, 3)
                for odd, ps in enumerate((psG, psO)):
                    nc.vector.tensor_copy(cq[:, odd:HEADS:2], ps[:, 256 + odd:256 + HEADS:2])
                nc.vector.tensor_tensor(row_out_b[:], psO[:, 0:P], row_out_b[:], ALU.add)
                dve.wait_ge(su_pe, 6)
                nc.vector.tensor_tensor(ffn_wt[:], psX[0][:, 0:P], ffn_wt[:], ALU.add)

        STEPS = HEADS + 2
        TAIL = {
            0: ["n1T"], 1: ["ffn1"], 2: ["nT"], 3: ["dt", "xc0", "xc1"], 4: ["xc2", "xc3"], 6: ["z0", "z1"],
            7: ["xdt0", "xdt1", "bc0", "bc1", "bc2"], 8: ["da0", "da1"], 9: ["y0"], 10: ["da2", "da3"],
            11: ["y1"], 12: ["ss", "mo"], 13: ["h3T"], 14: ["g0", "g1", "g2", "g3"], 15: ["mlp"],
            16: ["n4T"], 17: ["ffn2"]}

        def pv_pair(step):
            return (step - 3) // 2 if step >= 3 and step % 2 else None

        def iteration(ia, it, block):
            att, tail = ia is not None, it is not None
            uses = []
            for step in range(STEPS):
                if att and pv_pair(step) is not None:
                    uses.append(f"r{pv_pair(step)}")
                if tail:
                    uses += TAIL.get(step, [])
            order = {name: n for n, name in enumerate(uses)}

            def X(name):
                return psX[order[name] % 2]

            def fill(pe, name):
                n = order[name]
                if n >= 2:
                    pe.wait_ge(misc_free[n % 2], n // 2)
                return psX[n % 2]

            def full(name):
                return misc_full[order[name] % 2]

            def free(name):
                return misc_free[order[name] % 2]

            def count(name):
                return order[name] // 2 + 1

            def wait_full(eng, name):
                eng.wait_ge(full(name), count(name))
                return X(name)

            def wait_read(eng, name):
                eng.wait_ge(free(name), count(name))

            @block.sync
            def _(sp):
                if att:
                    sp.dma_start(xin[:], a["x"][ia].rearrange("(t p) e -> p t e", p=P)).then_inc(s["x_loaded"], 16)
                if tail:
                    wait_read(sp, "ffn2")
                    sp.dma_start(out[it].rearrange("(t p) e -> p t e", p=P), x4[:]).then_inc(s["out_dma"], 16)
                    sp.wait_ge(s["out_dma"], 16)

            def three_passes(ps, lhs, rhs):
                (lh, ll), (rh, rl) = lhs, rhs
                nc.tensor.matmul(ps, lh, rh, start=True, stop=False)
                nc.tensor.matmul(ps, lh, rl, start=False, stop=False)
                return nc.tensor.matmul(ps, ll, rh, start=False, stop=True)

            def wait_pt(eng, h, t):
                if t == 0:
                    eng.wait_ge(s["pt_act"], h + 1)
                else:
                    eng.wait_ge(s["pt_dve"], 3 * h + t)

            @block.tensor
            def _(pe):
                def project_g(h):
                    if h == 0:
                        pe.wait_ge(s["hT_ready"], 1)
                    else:
                        pe.wait_ge(s["g_evac"], h)
                    three_passes(psG[:], (mh[:, h, :], ml[:, h, :]), (hTh[:], hTl[:])).then_inc(s["g_full"], 1)

                def begin():
                    pe.wait_ge(s["xn_ready"], NT)
                    for t in range(NT):
                        last = nc.tensor.transpose(psG[:, P * t:P * t + P], xn[:, t, :], ident)
                    last.then_inc(s["xnT_full"], 1)
                    pe.wait_ge(s["hTh_ready"], 1)
                    pe.wait_ge(s["hTl_ready"], 1)
                    project_g(0)
                    for v in range(2 * NT):
                        t, half = v // 2, v % 2
                        if v >= 4:
                            pe.wait_ge(s["v_evac_dve" if v % 2 else "v_evac_act"], (v - 4) // 2 + 1)
                        cols = slice(512 * half, 512 * half + 512)
                        three_passes((psS + psT)[v % 4][:], (hTh[:, P * t:P * t + P], hTl[:, P * t:P * t + P]),
                                     (wvh[:, cols], wvl[:, cols])).then_inc(s["v_full"], 1)

                def scores(h, t):
                    n = NT * h + t
                    if n >= 2:
                        pe.wait_ge(s["sm_ready"], n - 1)
                    elif n == 0:
                        pe.wait_ge(s["v_evac_act"], NT)
                        pe.wait_ge(s["v_evac_dve"], NT)
                    if t == 0:
                        pe.wait_ge(s["gh_ready"], h + 1)
                        pe.wait_ge(s["gl_ready"], h + 1)
                    w = tile_cols(t)
                    q = slice(P * t, P * t + P)
                    three_passes(psS[n % 2][:, 0:w], (Gh[h % 2][:, q], Gl[h % 2][:, q]),
                                 (hTh[:, 0:w], hTl[:, 0:w])).then_inc(s["s_full"], 1)

                def turn(h, t):
                    n = NT * h + t
                    if n >= 2:
                        wait_pt(pe, (n - 2) // NT, (n - 2) % NT)
                    pe.wait_ge(s["p_ready"], n + 1)
                    for j in range(t + 1):
                        last = nc.tensor.transpose(psT[n % 2][:, P * j:P * j + P],
                                                   Pr[h % 2][:, TRI_AT[t] + P * j:TRI_AT[t] + P * j + P], ident)
                    last.then_inc(s["t_full"], 1)

                def attend(p):
                    ps = fill(pe, f"r{p}")
                    pe.wait_ge(s["spread_ready"], p + 1)
                    for t in range(NT):
                        last = nc.tensor.transpose(ps[:, P * t:P * t + P], R[:, P * t:P * t + P], ident)
                    last.then_inc(full(f"r{p}"), 1)
                    wait_pt(pe, 2 * p + 1, 0)
                    wait_pt(pe, 2 * p + 1, NT - 1)
                    if p >= 1:
                        pe.wait_ge(s["o_ready"], p)
                    for j in range(NT):
                        for hh in range(2):
                            h = 2 * p + hh
                            last = nc.tensor.matmul(psO[HD * hh:HD * hh + HD, P * j:TOK], V[:, j, HD * h:HD * h + HD],
                                                    PT[h % 4][:, j, P * j:TOK], start=(j == 0), stop=(j == NT - 1),
                                                    skip_group_check=True)
                    last.then_inc(s["pv_done"], 1)

                def project_out():
                    pe.wait_ge(s["o_ready"], PAIRS)
                    pe.wait_ge(s["g_evac"], HEADS)
                    for t in range(NT):
                        for p in range(PAIRS):
                            last = nc.tensor.matmul(psG[:, P * t:P * t + P], V[:, t, P * p:P * p + P], wo[:, p, :],
                                                    start=(p == 0), stop=(p == PAIRS - 1), skip_group_check=True)
                    last.then_inc(s["y_full"], 1)

                def transposed(name, src):
                    ps = fill(pe, name)
                    for t in range(NT):
                        last = nc.tensor.transpose(ps[:, P * t:P * t + P], src[:, t, :], ident)
                    last.then_inc(full(name), 1)

                def linear(name, lhsT, w):
                    ps = fill(pe, name)
                    for t in range(NT):
                        last = nc.tensor.matmul(ps[:, P * t:P * t + P], lhsT[:, P * t:P * t + P], w, start=True, stop=True)
                    last.then_inc(full(name), 1)

                def channels(name, w):
                    ps = fill(pe, name)
                    nc.tensor.matmul(ps[:], w, nT[:], start=True, stop=True).then_inc(full(name), 1)

                def tail_part(step):
                    if step == 0:
                        pe.wait_ge(s["n1_ready"], NT)
                        transposed("n1T", n1)
                    elif step == 1:
                        wait_read(pe, "n1T")
                        linear("ffn1", n1T, ffn_wt[:])
                    elif step == 2:
                        pe.wait_ge(s["n_ready"], NT)
                        transposed("nT", nn)
                    elif step == 3:
                        wait_read(pe, "nT")
                        ps = fill(pe, "dt")
                        for t in range(NT):
                            last = nc.tensor.matmul(ps[:, MHEADS * t:MHEADS * t + MHEADS], nT[:, P * t:P * t + P],
                                                    win_t[:, 768:772], start=True, stop=True)
                        last.then_inc(full("dt"), 1)
                        channels("xc0", win_t[:, 256:384])
                        channels("xc1", win_t[:, 384:512])
                    elif step == 4:
                        channels("xc2", win_t[:, 512:640])
                        channels("xc3", win_t[:, 640:768])
                    elif step == 6:
                        channels("z0", win_t[:, 0:128])
                        channels("z1", win_t[:, 128:256])
                    elif step == 7:
                        pe.wait_ge(s["silu_ready"], 4)
                        for k in range(2):
                            ps = fill(pe, f"xdt{k}")
                            for tt in range(2):
                                for c in range(2):
                                    t = 2 * k + tt
                                    last = nc.tensor.transpose(ps[:, INNER * tt + P * c:INNER * tt + P * c + P],
                                                               xbc[:, c, P * t:P * t + P], ident)
                            last.then_inc(full(f"xdt{k}"), 1)
                        for k, js in enumerate(BC_TILES):
                            ps = fill(pe, f"bc{k}")
                            at = 0
                            for j in js:
                                w = TOK - P * j
                                last = nc.tensor.matmul(ps[:, at:at + w], xbc[:, 2, P * j:P * j + P],
                                                        xbc[:, 3, P * j:TOK], start=True, stop=True)
                                at += w
                            last.then_inc(full(f"bc{k}"), 1)
                    elif step in (8, 10):
                        pe.wait_ge(s["da_ready"], 1)
                        for h in (0, 1) if step == 8 else (2, 3):
                            ps = fill(pe, f"da{h}")
                            for t in range(NT):
                                k = MHEADS * t + h
                                last = nc.tensor.transpose(ps[:, P * t:P * t + P], dA[:, k:k + 1].to_broadcast([P, P]),
                                                           ident)
                            last.then_inc(full(f"da{h}"), 1)
                    elif step in (9, 11):
                        p = (step - 9) // 2
                        ps = fill(pe, f"y{p}")
                        for k in range(2):
                            wait_read(pe, f"xdt{k}")
                        pe.wait_ge(s["m_ready"], 2 * p + 2)
                        for j in range(NT):
                            for hh in range(2):
                                h = 2 * p + hh
                                last = nc.tensor.matmul(ps[HD * hh:HD * hh + HD, P * j:TOK], xdt[:, j, HD * h:HD * h + HD],
                                                        M[h % 2][:, COL_AT[j]:COL_AT[j] + TOK - P * j], start=(j == 0),
                                                        stop=(j == NT - 1), skip_group_check=True)
                        last.then_inc(full(f"y{p}"), 1)
                    elif step == 12:
                        ps = fill(pe, "ss")
                        pe.wait_ge(s["y2_ready"], 2)
                        for t in range(NT):
                            for c in range(2):
                                last = nc.tensor.matmul(ps[:, t:t + 1], y2[:, c, P * t:P * t + P], ones[:],
                                                        start=(c == 0), stop=(c == 1), skip_group_check=True)
                        last.then_inc(full("ss"), 1)
                        ps = fill(pe, "mo")
                        for t in range(NT):
                            for c in range(2):
                                last = nc.tensor.matmul(ps[:, P * t:P * t + P], yz[:, c, P * t:P * t + P], wmo[:, c, :],
                                                        start=(c == 0), stop=(c == 1), skip_group_check=True)
                        last.then_inc(full("mo"), 1)
                    elif step == 13:
                        pe.wait_ge(s["h3_ready"], NT)
                        transposed("h3T", h3)
                    elif step == 14:
                        wait_read(pe, "h3T")
                        for f in range(4):
                            ps = fill(pe, f"g{f}")
                            nc.tensor.matmul(ps[:], w1[:, P * f:P * f + P], h3T, start=True,
                                             stop=True).then_inc(full(f"g{f}"), 1)
                    elif step == 15:
                        ps = fill(pe, "mlp")
                        for f in range(4):
                            wait_read(pe, f"g{f}")
                        for t in range(NT):
                            for f in range(4):
                                last = nc.tensor.matmul(ps[:, P * t:P * t + P], gl[:, f, P * t:P * t + P], w2[:, f, :],
                                                        start=(f == 0), stop=(f == 3), skip_group_check=True)
                        last.then_inc(full("mlp"), 1)
                    elif step == 16:
                        pe.wait_ge(s["n4_ready"], NT)
                        transposed("n4T", n4)
                    elif step == 17:
                        wait_read(pe, "n4T")
                        linear("ffn2", n4T, ffn_wt[:])

                if att:
                    begin()
                for step in range(STEPS):
                    if att:
                        for t in range(NT):
                            if step < HEADS:
                                scores(step, t)
                            if 1 <= step <= HEADS:
                                turn(step - 1, t)
                            if t == 1 and step + 1 < HEADS:
                                project_g(step + 1)
                        if pv_pair(step) is not None:
                            attend(pv_pair(step))
                    if tail:
                        tail_part(step)
                if att:
                    project_out()

            @block.scalar
            def _(act):
                def begin():
                    act.wait_ge(s["xnT_full"], 1)
                    nc.scalar.copy(hT[:], psG[:]).then_inc(s["hT_ready"], 1)

                def copy_g(h):
                    act.wait_ge(s["g_full"], h + 1)
                    if h >= 1:
                        act.wait_ge(s["gh_ready"], h)
                        act.wait_ge(s["gl_ready"], h)
                    nc.scalar.activation(G[:], psG[:], ACT.Identity, bias=cq[:, h:h + 1]).then_inc(s["g_evac"], 1)

                def copy_v():
                    for v in range(0, 2 * NT, 2):
                        act.wait_ge(s["v_full"], v + 1)
                        nc.scalar.copy(V[:, v // 2, 0:512], (psS + psT)[v % 4][:]).then_inc(s["v_evac_act"], 1)

                def probs(h, t):
                    n = NT * h + t
                    act.wait_ge(s["sm_ready"], n + 1)
                    if h >= 2:
                        act.wait_ge(s["t_full"], n - 2 * NT + 1)
                    w = tile_cols(t)
                    nc.scalar.activation(Pr[h % 2][:, TRI_AT[t]:TRI_AT[t] + w], Sm[n % 3][:, 0:w], ACT.Exp,
                                         bias=nb[:, n:n + 1], scale=-1.0,
                                         accum_out=den[:, h, t:t + 1]).then_inc(s["p_ready"], 1)

                def copy_t0(h):
                    act.wait_ge(s["t_full"], NT * h + 1)
                    if h >= 4:
                        act.wait_ge(s["pv_done"], (h - 4) // 2 + 1)
                    nc.scalar.copy(PT[h % 4][:, 0, 0:P], psT[NT * h % 2][:, 0:P]).then_inc(s["pt_act"], 1)

                def copy_r(p):
                    if p >= 1:
                        act.wait_ge(s["o_ready"], p)
                    evacuate(R[:], f"r{p}")

                def evacuate(dst, name):
                    ps = wait_full(act, name)
                    nc.scalar.copy(dst, ps[:]).then_inc(free(name), 1)

                def tail_part(step):
                    if step == 0:
                        evacuate(n1T[:], "n1T")
                    elif step == 2:
                        evacuate(nT[:], "nT")
                    elif step in (3, 4):
                        for c in (0, 1) if step == 3 else (2, 3):
                            evacuate(pad[:, c, CONV - 1:], f"xc{c}")
                    elif step == 5:
                        act.wait_ge(s["dt_abs"], 1)
                        nc.scalar.activation(dt_exp[:], dt_abs[:], ACT.Exp, scale=-1.0).then_inc(s["dt_exp"], 1)
                    elif step == 6:
                        for c in range(4):
                            act.wait_ge(s["conv_ready"], c + 1)
                            nc.scalar.activation(xbc[:, c, :], acc[c], ACT.Silu).then_inc(s["silu_ready"], 1)
                        for c in range(2):
                            ps = wait_full(act, f"z{c}")
                            nc.scalar.activation(zs[:, c, :], ps[:], ACT.Silu).then_inc(free(f"z{c}"), 1)
                    elif step == 7:
                        act.wait_ge(s["dta_ready"], 1)
                        nc.scalar.activation(dA[:], dta[:], ACT.Exp).then_inc(s["da_ready"], 1)
                        for k, js in enumerate(BC_TILES):
                            ps = wait_full(act, f"bc{k}")
                            at = 0
                            for j in js:
                                w = TOK - P * j
                                last = nc.scalar.copy(bc[:, COL_AT[j]:COL_AT[j] + w], ps[:, at:at + w])
                                at += w
                            last.then_inc(free(f"bc{k}"), 1)
                    elif step in (9, 11):
                        c = (step - 9) // 2
                        act.wait_ge(s["yz_ready"], c + 1)
                        nc.scalar.activation(y2[:, c, :], yz[:, c, :], ACT.Square).then_inc(s["y2_ready"], 1)
                    elif step == 12:
                        wait_read(act, "mo")
                        for t in range(NT):
                            nc.scalar.activation(usq[:, t, :], u2[:, t, :], ACT.Square,
                                                 accum_out=ss2[:, t:t + 1]).then_inc(s["ss2_ready"], 1)
                    elif step == 13:
                        evacuate(h3T, "h3T")
                    elif step == 14:
                        for f in range(4):
                            ps = wait_full(act, f"g{f}")
                            nc.scalar.activation(gl[:, f, :], ps[:], ACT.Gelu,
                                                 bias=b1[:, f:f + 1]).then_inc(free(f"g{f}"), 1)
                    elif step == 16:
                        evacuate(n4T[:], "n4T")

                if att:
                    begin()
                    copy_g(0)
                    copy_v()
                for step in range(STEPS):
                    if att:
                        for t in range(NT):
                            if step < HEADS:
                                probs(step, t)
                            if t == 0 and 1 <= step <= HEADS:
                                copy_t0(step - 1)
                            if t == 1 and step + 1 < HEADS:
                                copy_g(step + 1)
                        if pv_pair(step) is not None:
                            copy_r(pv_pair(step))
                    if tail:
                        tail_part(step)

            @block.vector
            def _(dve):
                chained = [0]

                def chain(last):
                    chained[0] += 1
                    last.then_inc(s["dve_chain"], 1)
                    dve.wait_ge(s["dve_chain"], chained[0])

                def statistics(x, stats, mv, ready):
                    for t in range(NT):
                        last = nc.vector.bn_stats(stats[:, t, :], x[:, t, :])
                    chain(last)
                    for t in range(NT):
                        last = nc.vector.bn_aggr(mv[:, t, :], stats[:, t, :])
                    last.then_inc(ready, 1)

                def normalise(dst, x, mv, rstd, ready):
                    for t in range(NT):
                        nc.vector.tensor_scalar(dst[:, t, :], x[:, t, :], mv[:, t, 0:1], rstd[:, t:t + 1],
                                                ALU.subtract, ALU.mult).then_inc(ready, 1)

                def begin():
                    dve.wait_ge(s["x_loaded"], 16)
                    statistics(xin, x_st, x_mv, s["x_mv"])
                    dve.wait_ge(s["x_mv"], 1)
                    dve.wait_ge(s["x_rstd"], 1)
                    normalise(xn, xin, x_mv, x_rstd, s["xn_ready"])

                def split_h():
                    dve.wait_ge(s["hT_ready"], 1)
                    nc.vector.tensor_copy(hTh[:], hT[:]).then_inc(s["hTh_ready"], 1)
                    dve.wait_ge(s["hTh_ready"], 1)
                    nc.vector.tensor_tensor(hTl[:], hT[:], hTh[:].bitcast(F32), ALU.subtract).then_inc(s["hTl_ready"], 1)

                def copy_v():
                    for v in range(1, 2 * NT, 2):
                        dve.wait_ge(s["v_full"], v + 1)
                        nc.vector.tensor_copy(V[:, v // 2, 512:1024], (psS + psT)[v % 4][:]).then_inc(s["v_evac_dve"], 1)

                def split_g(h):
                    dve.wait_ge(s["g_evac"], h + 1)
                    if h >= 2:
                        dve.wait_ge(s["s_full"], NT * (h - 1))
                        dve.wait_ge(s["gl_ready"], h - 1)
                    nc.vector.tensor_copy(Gh[h % 2][:], G[:]).then_inc(s["gh_ready"], 1)

                def mask_and_max(h, t):
                    n = NT * h + t
                    dve.wait_ge(s["s_full"], n + 1)
                    if n >= 3:
                        dve.wait_ge(s["p_ready"], n - 2)
                    w = tile_cols(t)
                    nc.vector.tensor_tensor_reduce(
                        out=Sm[n % 3][:, 0:w], in0=psS[n % 2][:, 0:w], in1=mask[:, TOK - w:TOK], scale=-SCALE,
                        scalar=3.0e38, op0=ALU.add, op1=ALU.min, accum_out=nb[:, n:n + 1]).then_inc(s["sm_ready"], 1)

                def copy_t(h, t):
                    dve.wait_ge(s["t_full"], NT * h + t + 1)
                    if h >= 4:
                        dve.wait_ge(s["pv_done"], (h - 4) // 2 + 1)
                    w = tile_cols(t)
                    src = psT[(NT * h + t) % 2][:, 0:w].rearrange("p (j q) -> p j q", q=P)
                    nc.vector.tensor_copy(PT[h % 4][:, 0:t + 1, P * t:P * t + P], src).then_inc(s["pt_dve"], 1)

                def invert(p):
                    dve.wait_ge(s["p_ready"], NT * (2 * p + 2))
                    nc.vector.reciprocal(rden[:, 2 * p:2 * p + 2, :], den[:, 2 * p:2 * p + 2, :]).then_inc(s["rden_ready"], 1)

                def normalise_o(p):
                    dve.wait_ge(s["pv_done"], p + 1)
                    wait_read(dve, f"r{p}")
                    nc.vector.tensor_tensor(V[:, :, P * p:P * p + P], psO[:].rearrange("p (t q) -> p t q", q=P),
                                            R[:].rearrange("p (t q) -> p t q", q=P), ALU.mult).then_inc(s["o_ready"], 1)

                def end():
                    dve.wait_ge(s["y_full"], 1)
                    dve.wait_ge(s["xb_ready"], NT)
                    if tail:
                        dve.wait_ge(s["n1_ready"], NT)
                        dve.wait_ge(s["x1b_ready"], NT)
                    nc.vector.tensor_tensor(x1[:].rearrange("p t e -> p (t e)"), psG[:],
                                            xin[:].rearrange("p t e -> p (t e)"), ALU.add).then_inc(s["x1_ready"], 1)
                    dve.wait_ge(s["x1_ready"], 1)

                def flat(x):
                    return x[:, :, :].rearrange("p t e -> p (t e)")

                def add_to(dst, name, x, ready, n):
                    ps = wait_full(dve, name)
                    dve.wait_ge(ready, n)
                    nc.vector.tensor_tensor(flat(dst), ps[:], flat(x), ALU.add).then_inc(free(name), 1)
                    wait_read(dve, name)

                def convolve(c):
                    wait_read(dve, f"xc{c}")
                    chain(nc.vector.tensor_scalar(acc[c], pad[:, c, CONV - 1:CONV - 1 + TOK],
                                                  conv_w[:, c, CONV - 1:CONV], conv_b[:, c:c + 1], ALU.mult, ALU.add))
                    for k in range(CONV - 1):
                        last = nc.vector.scalar_tensor_tensor(
                            out=acc[c], in0=pad[:, c, k:k + TOK], scalar=conv_w[:, c, k:k + 1], in1=acc[c],
                            op0=ALU.mult, op1=ALU.add)
                        if k < CONV - 2:
                            chain(last)
                        else:
                            last.then_inc(s["conv_ready"], 1)

                def tail_begin():
                    statistics(x1, st, a_mv, s["a_mv"])
                    dve.wait_ge(s["a_mv"], 1)
                    dve.wait_ge(s["a_rstd"], 1)
                    normalise(n1, x1, a_mv, a_rstd, s["n1_ready"])

                def tail_part(step):
                    if step == 1:
                        add_to(x2, "ffn1", x1b, s["x1b_ready"], NT)
                        statistics(x2, st2, b_mv, s["b_mv"])
                        dve.wait_ge(s["b_mv"], 1)
                        dve.wait_ge(s["b_r12"], 1)
                        for t in range(NT):
                            nc.vector.tensor_scalar(u[:, t, :], x2[:, t, :], b_mv[:, t, 0:1], b_r1[:, t:t + 1],
                                                    ALU.subtract, ALU.mult)
                        normalise(nn, x2, b_mv, b_r12, s["n_ready"])
                    elif step == 3:
                        ps = wait_full(dve, "dt")
                        nc.vector.tensor_tensor(dtx[:], ps[:, 0:NT * MHEADS], dt_bias[:], ALU.add).then_inc(free("dt"), 1)
                    elif step in (4, 5):
                        for c in (0, 1) if step == 4 else (2, 3):
                            convolve(c)
                    elif step == 7:
                        dve.wait_ge(s["dt_ready"], 1)
                        for k in range(2):
                            ps = wait_full(dve, f"xdt{k}")
                            nc.vector.tensor_tensor(
                                xdt[:, 2 * k:2 * k + 2, :].rearrange("p t (h d) -> p (t h) d", d=HD),
                                ps[:].rearrange("p (g d) -> p g d", d=HD),
                                dt[:, 8 * k:8 * k + 8].unsqueeze(2).to_broadcast([P, 8, HD]),
                                ALU.mult).then_inc(free(f"xdt{k}"), 1)
                    elif step in (8, 10):
                        for h in (0, 1) if step == 8 else (2, 3):
                            ps = wait_full(dve, f"da{h}")
                            if h >= 2:
                                dve.wait_ge(s["m_ready"], h - 1)
                            for j in range(NT):
                                w = TOK - P * j
                                last = nc.vector.tensor_tensor_scan(
                                    L[h % 2][:, COL_AT[j]:COL_AT[j] + w], ps[:, P * j:TOK], eye_row[:, 0:w], 0.0,
                                    ALU.mult, ALU.add)
                            last.then_inc(free(f"da{h}"), 1)
                    elif step in (9, 11):
                        c = (step - 9) // 2
                        ps = wait_full(dve, f"y{c}")
                        nc.vector.scalar_tensor_tensor(out=yd[:, c, :], in0=xbc[:, c, :], scalar=d_col[:, c:c + 1],
                                                       in1=ps[:], op0=ALU.mult, op1=ALU.add).then_inc(free(f"y{c}"), 1)
                        wait_read(dve, f"y{c}")
                        wait_read(dve, f"z{c}")
                        nc.vector.tensor_tensor(yz[:, c, :], yd[:, c, :], zs[:, c, :], ALU.mult).then_inc(s["yz_ready"], 1)
                    elif step == 12:
                        ps = wait_full(dve, "ss")
                        nc.vector.tensor_scalar(ss[:], ps[:, 0:NT], 1.0 / INNER, LN_EPS, ALU.mult,
                                                ALU.add).then_inc(free("ss"), 1)
                        dve.wait_ge(s["rs_ready"], 1)
                        ps = wait_full(dve, "mo")
                        for t in range(NT):
                            last = nc.vector.scalar_tensor_tensor(
                                out=u2[:, t, :], in0=ps[:, P * t:P * t + P], scalar=rs[:, t:t + 1], in1=u[:, t, :],
                                op0=ALU.mult, op1=ALU.add)
                        last.then_inc(free("mo"), 1)
                        wait_read(dve, "mo")
                        dve.wait_ge(s["r3_ready"], 1)
                        for t in range(NT):
                            nc.vector.tensor_scalar(h3[:, t, :], u2[:, t, :], r3[:, t:t + 1], None,
                                                    ALU.mult).then_inc(s["h3_ready"], 1)
                    elif step == 15:
                        add_to(x3, "mlp", x2b, s["x2b_ready"], 1)
                        statistics(x3, st4, d_mv, s["d_mv"])
                        dve.wait_ge(s["d_mv"], 1)
                        dve.wait_ge(s["d_rstd"], 1)
                        normalise(n4, x3, d_mv, d_rstd, s["n4_ready"])
                    elif step == 17:
                        add_to(x4, "ffn2", x3b, s["x3b_ready"], NT)

                if att:
                    begin()
                if tail:
                    tail_begin()
                if att:
                    split_h()
                    split_g(0)
                    copy_v()
                for step in range(STEPS):
                    if att:
                        if step >= 2 and step % 2 == 0 and step <= HEADS:
                            invert(step // 2 - 1)
                        for t in range(NT):
                            if step < HEADS:
                                mask_and_max(step, t)
                            if t >= 1 and 1 <= step <= HEADS:
                                copy_t(step - 1, t)
                            if t == 2 and step + 1 < HEADS:
                                split_g(step + 1)
                        if pv_pair(step) is not None:
                            normalise_o(pv_pair(step))
                    if tail:
                        tail_part(step)
                if att:
                    end()

            @block.gpsimd
            def _(pool):
                chained = [0]

                def chain(last):
                    chained[0] += 1
                    last.then_inc(s["pool_chain"], 1)
                    pool.wait_ge(s["pool_chain"], chained[0])

                def inverse_deviation(mv, veps, rstd, mv_ready, ready):
                    pool.wait_ge(mv_ready, 1)
                    chain(nc.gpsimd.tensor_scalar(veps[:], mv[:, :, 1], LN_EPS, None, ALU.add))
                    nc.gpsimd.tensor_tensor(rstd[:], veps[:], neg_half[:], ALU.pow).then_inc(ready, 1)

                def add_rows(dst, x, row, ready):
                    for t in range(NT):
                        nc.gpsimd.tensor_tensor(dst[:, t, :], x[:, t, :], row[:], ALU.add).then_inc(ready, 1)

                def split_g(h):
                    pool.wait_ge(s["gh_ready"], h + 1)
                    if h >= 2:
                        pool.wait_ge(s["s_full"], NT * (h - 1))
                    nc.gpsimd.tensor_tensor(Gl[h % 2][:], G[:], Gh[h % 2][:].bitcast(F32),
                                            ALU.subtract).then_inc(s["gl_ready"], 1)

                def spread(p):
                    pool.wait_ge(s["rden_ready"], p + 1)
                    if p >= 1:
                        pool.wait_ge(s["o_ready"], p)
                    for t in range(NT):
                        last = nc.gpsimd.tensor_copy(R[:, P * t:P * t + P].rearrange("p (h d) -> p h d", d=HD),
                                                     rden[:, 2 * p:2 * p + 2, t:t + 1].to_broadcast([P, 2, HD]))
                    last.then_inc(s["spread_ready"], 1)

                def softplus():
                    wait_read(pool, "dt")
                    chain(nc.gpsimd.tensor_scalar(dt_s[:], dtx[:], 0.0, 2.0, ALU.max, ALU.mult))
                    nc.gpsimd.tensor_tensor(dt_abs[:], dt_s[:], dtx[:], ALU.subtract).then_inc(s["dt_abs"], 1)

                def softplus_end():
                    pool.wait_ge(s["dt_exp"], 1)
                    chain(nc.gpsimd.tensor_scalar(dt_s[:], dt_exp[:], 2.0, None, ALU.add))
                    chain(nc.gpsimd.tensor_tensor(dt_s2[:], dt_s[:], neg_one[:], ALU.pow))
                    chain(nc.gpsimd.tensor_tensor(dt_s[:], dt_exp[:], dt_s2[:], ALU.mult))
                    chain(nc.gpsimd.tensor_tensor(dt_s2[:], dt_s[:], dt_s[:], ALU.mult))
                    coef = [2.0 / (2 * k + 1) for k in range(LOG_TERMS)]
                    chain(nc.gpsimd.tensor_scalar(dt_poly[:], dt_s2[:], coef[-1], coef[-2], ALU.mult, ALU.add))
                    for k in range(LOG_TERMS - 3, -1, -1):
                        chain(nc.gpsimd.tensor_tensor(dt_poly[:], dt_poly[:], dt_s2[:], ALU.mult))
                        chain(nc.gpsimd.tensor_scalar(dt_poly[:], dt_poly[:], coef[k], None, ALU.add))
                    chain(nc.gpsimd.tensor_tensor(dt_poly[:], dt_poly[:], dt_s[:], ALU.mult))
                    chain(nc.gpsimd.tensor_scalar(dt_s[:], dtx[:], 0.0, None, ALU.max))
                    nc.gpsimd.tensor_tensor(dt[:], dt_s[:], dt_poly[:], ALU.add).then_inc(s["dt_ready"], 1)
                    pool.wait_ge(s["dt_ready"], 1)
                    nc.gpsimd.tensor_tensor(dta[:], dt[:], neg_a[:], ALU.mult).then_inc(s["dta_ready"], 1)

                def tail_part(step):
                    if step == 1:
                        pool.wait_ge(s["b_mv"], 1)
                        chain(nc.gpsimd.tensor_scalar(b_veps[:], b_mv[:, :, 1], LN_EPS, None, ALU.add))
                        chain(nc.gpsimd.tensor_tensor(b_r1[:], b_veps[:], neg_half[:], ALU.pow))
                        chain(nc.gpsimd.tensor_tensor(b_sq[:], b_r1[:], b_r1[:], ALU.mult))
                        chain(nc.gpsimd.tensor_tensor(b_sq[:], b_sq[:], b_mv[:, :, 1], ALU.mult))
                        chain(nc.gpsimd.tensor_scalar(b_sq[:], b_sq[:], float(P), BN_EPS, ALU.mult, ALU.add))
                        chain(nc.gpsimd.tensor_tensor(b_r2[:], b_sq[:], neg_half[:], ALU.pow))
                        nc.gpsimd.tensor_tensor(b_r12[:], b_r1[:], b_r2[:], ALU.mult).then_inc(s["b_r12"], 1)
                    elif step == 4:
                        softplus()
                    elif step == 5:
                        softplus_end()
                    elif step in (8, 10):
                        for h in (0, 1) if step == 8 else (2, 3):
                            for k in range(len(BC_TILES)):
                                wait_read(pool, f"bc{k}")
                            wait_read(pool, f"da{h}")
                            if h >= 2:
                                pool.wait_ge(full("y0"), count("y0"))
                            nc.gpsimd.tensor_tensor(M[h % 2], L[h % 2], bc[:], ALU.mult).then_inc(s["m_ready"], 1)
                    elif step == 12:
                        wait_read(pool, "ss")
                        nc.gpsimd.tensor_tensor(rs[:], ss[:], neg_half[:], ALU.pow).then_inc(s["rs_ready"], 1)
                        pool.wait_ge(s["ss2_ready"], NT)
                        chain(nc.gpsimd.tensor_scalar(r3_eps[:], ss2[:], BN_EPS, None, ALU.add))
                        nc.gpsimd.tensor_tensor(r3[:], r3_eps[:], neg_half[:], ALU.pow).then_inc(s["r3_ready"], 1)
                        for t in range(NT):
                            last = nc.gpsimd.tensor_tensor(x2b[:, t, :], x2[:, t, :], u2[:, t, :], ALU.add)
                        chain(last)
                        for t in range(NT):
                            last = nc.gpsimd.tensor_tensor(x2b[:, t, :], x2b[:, t, :], b2[:], ALU.add)
                        last.then_inc(s["x2b_ready"], 1)
                    elif step == 15:
                        inverse_deviation(d_mv, d_veps, d_rstd, s["d_mv"], s["d_rstd"])
                        add_rows(x3b, x3, ffn_b, s["x3b_ready"])

                if att:
                    inverse_deviation(x_mv, x_veps, x_rstd, s["x_mv"], s["x_rstd"])
                if tail:
                    inverse_deviation(a_mv, a_veps, a_rstd, s["a_mv"], s["a_rstd"])
                    add_rows(x1b, x1, ffn_b, s["x1b_ready"])
                if att:
                    pool.wait_ge(s["xn_ready"], NT)
                    add_rows(xin, xin, row_out_b, s["xb_ready"])
                    split_g(0)
                for step in range(STEPS):
                    if att and step + 1 < HEADS:
                        split_g(step + 1)
                    if att and step >= 2 and step % 2 == 0 and step <= HEADS:
                        spread(step // 2 - 1)
                    if tail:
                        tail_part(step)

        batch = a["x"].shape[0]
        with nc.Block() as block:
            iteration(0, None, block)
        nc.all_engine_barrier(sems_to_clear=loop_sems)
        with nc.Fori(1, batch) as i:
            with nc.Block() as block:
                iteration(i, i - 1, block)
            nc.all_engine_barrier(sems_to_clear=loop_sems)
        with nc.Block() as block:
            iteration(None, batch - 1, block)


def kernel(**inputs):
    import concourse.bacc as bacc
    from concourse.bass_utils import run_bass_kernel_spmd

    g = {k: np.asarray(v) for k, v in inputs.items()}
    w = g["L0_attn_a_qkv_w"].transpose(1, 2, 0)

    def pairs(m):
        return m.reshape(PAIRS, P, -1).transpose(1, 0, 2)

    def columns(v):
        return v.reshape(-1, P).T

    def rows(v, times=1):
        return np.tile(v.reshape(1, -1), (P, times))

    eye = np.eye(P, dtype=np.float32)
    causal = np.zeros((P, TOK), np.float32)
    causal[:, TOK - P:] = np.triu(np.full((P, P), MASKED, np.float32), 1)
    eye_row = np.zeros((P, TOK), np.float32)
    eye_row[:, :P] = eye
    arrays = {
        "x": g["L0_attn_a_x"],
        "wq_t": pairs(w[:, 0:HD]), "wk_t": pairs(w[:, HD:2 * HD]),
        "wv": g["L0_attn_a_qkv_w"][:, :, 2 * HD:].reshape(P, HEADS * HD),
        "wo": pairs(g["L0_attn_a_out_w"]),
        "bq": columns(g["L0_attn_a_qkv_b"][:, 0:HD]), "bv": columns(g["L0_attn_a_qkv_b"][:, 2 * HD:]),
        "out_b": rows(g["L0_attn_a_out_b"]),
        "ffn_wt": g["L0_ffn_W"].T, "ffn_b": rows(g["L0_ffn_b"]), "up_t": g["L0_ffn_up_aux"].T,
        "lora_up_t": g["L0_ffn_lora_up"].T, "lora_down_t": g["L0_ffn_lora_down"].T,
        "down_aux": g["L0_ffn_down_aux"],
        "norm1": g["L0_attn_b_norm1_w"].reshape(P, 1), "norm2": g["L0_attn_b_norm2_w"].reshape(P, 1),
        "win_t": g["L0_attn_b_in_proj_w"].T,
        "conv_w": g["L0_attn_b_conv_w"].reshape(4, P, CONV).transpose(1, 0, 2),
        "conv_b": columns(g["L0_attn_b_conv_b"]),
        "dt_bias": rows(g["L0_attn_b_dt_bias"], NT), "a_log": rows(g["L0_attn_b_A_log"], NT),
        "d_col": columns(np.repeat(g["L0_attn_b_D"], HD)), "mnorm": columns(g["L0_attn_b_mnorm_w"]),
        "wmo": g["L0_attn_b_out_proj_w"].T.reshape(2, P, P).transpose(1, 0, 2),
        "w1": g["L0_attn_b_mlp_w1"].T, "b1": columns(g["L0_attn_b_mlp_b1"]),
        "w2": g["L0_attn_b_mlp_w2"].T.reshape(4, P, P).transpose(1, 0, 2), "b2": rows(g["L0_attn_b_mlp_b2"]),
        "mask": causal, "eye_row": eye_row,
    }
    nc = bacc.Bacc("TRN2", target_bir_lowering=False, num_devices=1)
    aps, ins = {}, {}
    for name, arr in arrays.items():
        arr = np.ascontiguousarray(arr)
        ins[f"in_{name}"] = arr
        aps[name] = nc.dram_tensor(f"in_{name}", arr.shape, mybir.dt.from_np(arr.dtype), kind="ExternalInput").ap()
    out = nc.dram_tensor("out", arrays["x"].shape, F32, kind="ExternalOutput").ap()
    layer(nc, aps, out)
    r = run_bass_kernel_spmd(nc, [ins], core_ids=[0])
    return r.results[0]["out"]
```

```python
from contextlib import ExitStack

import numpy as np

import concourse.bass as bass
from concourse import mybir

F32 = mybir.dt.float32
F32R = mybir.dt.float32r
ALU = mybir.AluOpType
ACT = mybir.ActivationFunctionType

P = 128
TOK = 512
NT = TOK // P
HEADS = 16
HD = 64
PAIRS = HEADS // 2
TRI = NT * (NT + 1) // 2 * P
MHEADS = 4
INNER = 256
CONV = 4
LN_EPS = 1e-5
BN_EPS = 1e-6
SCALE = HD ** -0.5
MASKED = -0.7 * float(np.finfo(np.float32).max)
LOG_TERMS = 8

TRI_AT = [P * t * (t + 1) // 2 for t in range(NT)]
BC_TILES = ((0,), (1, 3), (2,))
COL_AT = [P * (NT * j - j * (j - 1) // 2) for j in range(NT)]

NAMES = """
x_loaded x_mv x_rstd xn_ready hTh_ready hTl_ready front_gh front_gl
xb_ready v_full v_evac
g_full g_evac gh_ready gl_ready s_full sm_ready p_ready t_full pt_act pt_dve
rden_ready spread_ready pv_done o_ready y_full x1_ready
misc_full0 misc_full1 misc_free0 misc_free1
dve_chain pool_chain
a_mv a_rstd n1_ready x1b_ready
b_mv b_r12 n_ready
dt_abs dt_exp dt_ready dta_ready da_ready
conv_ready tanh_ready ztanh_ready silu_ready m_ready
yz_ready y2_ready rs_ready ss2_ready r3_ready h3_ready x2b_ready
d_mv d_rstd n4_ready x3b_ready
out_dma
""".split()


def tile_cols(t):
    return P * (t + 1)


def layer(nc, a, out):
    with ExitStack() as ctx:
        def sb(name, shape, dt=F32):
            return ctx.enter_context(nc.sbuf_tensor(name, shape, dt))

        def bank(name):
            return ctx.enter_context(nc.psum_tensor(name, [P, 512], F32))

        psS = [bank("psS0"), bank("psS1")]
        psT = [bank("psT0"), bank("psT1")]
        psG = bank("psG")
        psO = bank("psO")
        psX = [bank("psX0"), bank("psX1")]

        mask = sb("mask", [P, TOK])
        eye_row = sb("eye_row", [P, TOK])
        ident = eye_row[:, 0:P]
        ones = sb("ones", [P, 1])
        neg_half = sb("neg_half", [P, NT])
        neg_one = sb("neg_one", [P, NT * MHEADS])
        PT = [sb(f"PT{i}", [P, NT, TOK]) for i in range(4)]
        wq_t = PT[0][:, 0:2, :].rearrange("p a (b e) -> p (a b) e", e=P)
        wk_t = PT[0][:, 2:4, :].rearrange("p a (b e) -> p (a b) e", e=P)
        wv = PT[1][:, 0:2, :].rearrange("p a c -> p (a c)")
        wo = sb("wo", [P, PAIRS, P])
        bq = sb("bq", [P, PAIRS])
        bv = sb("bv", [P, PAIRS])
        row_out_b = sb("row_out_b", [P, P])
        ffn_wt = sb("ffn_wt", [P, P])
        ffn_b = sb("ffn_b", [P, P])
        up_t = sb("up_t", [50, P])
        lora_up_t = sb("lora_up_t", [4, 50])
        lora_down_t = sb("lora_down_t", [100, 4])
        down_aux = sb("down_aux", [100, P])
        norm1 = sb("norm1", [P, 1])
        norm2 = sb("norm2", [P, 1])
        win_t = sb("win_t", [P, 772])
        conv_w = sb("conv_w", [P, 4, CONV])
        conv_b = sb("conv_b", [P, 4])
        dt_bias = sb("dt_bias", [P, NT * MHEADS])
        a_log = sb("a_log", [P, NT * MHEADS])
        d_col = sb("d_col", [P, 2])
        mnorm = sb("mnorm", [P, 2])
        wmo = sb("wmo", [P, 2, P])
        w1 = sb("w1", [P, 4 * P])
        b1 = sb("b1", [P, 4])
        w2 = sb("w2", [P, 4, P])
        b2 = sb("b2", [P, P])
        exp_a = sb("exp_a", [P, NT * MHEADS])
        lora1 = sb("lora1", [4, P])
        lora2 = sb("lora2", [50, P])
        cq = sb("cq", [P, HEADS])
        mh = sb("mh", [P, HEADS, P], F32R)
        ml = sb("ml", [P, HEADS, P], F32R)
        wvh = sb("wvh", [P, HEADS * HD], F32R)
        wvl = sb("wvl", [P, HEADS * HD], F32R)

        xin = sb("xin", [P, NT, P])
        x_st = sb("x_st", [P, NT, 6])
        x_mv = sb("x_mv", [P, NT, 2])
        x_veps = sb("x_veps", [P, NT])
        x_rstd = sb("x_rstd", [P, NT])
        xn = sb("xn", [P, NT, P])
        hT = xn[:].rearrange("p t e -> p (t e)")
        xb = sb("xb", [P, NT, P])
        hTh = sb("hTh", [P, TOK], F32R)
        hTl = sb("hTl", [P, TOK], F32R)
        V = sb("V", [P, NT, HEADS * HD])
        G = sb("G", [P, TOK])
        Gh = [sb(f"Gh{i}", [P, TOK], F32R) for i in range(2)]
        Gl = [sb(f"Gl{i}", [P, TOK], F32R) for i in range(2)]
        Sm = [sb(f"Sm{i}", [P, TOK]) for i in range(3)]
        nb = sb("nb", [P, HEADS * NT])
        den = sb("den", [P, HEADS, NT])
        rden = sb("rden", [P, HEADS, NT])
        Pr = [sb(f"Pr{i}", [P, TRI]) for i in range(2)]
        R = sb("R", [P, TOK])
        x1 = sb("x1", [P, NT, P])

        st = sb("st", [P, NT, 6])
        a_mv = sb("a_mv", [P, NT, 2])
        a_veps = sb("a_veps", [P, NT])
        a_rstd = sb("a_rstd", [P, NT])
        n1 = sb("n1", [P, NT, P])
        x1b = sb("x1b", [P, NT, P])
        n1T = sb("n1T", [P, TOK])
        x2 = sb("x2", [P, NT, P])
        st2 = sb("st2", [P, NT, 6])
        b_mv = sb("b_mv", [P, NT, 2])
        b_veps = sb("b_veps", [P, NT])
        b_r1 = sb("b_r1", [P, NT])
        b_sq = sb("b_sq", [P, NT])
        b_r2 = sb("b_r2", [P, NT])
        b_r12 = sb("b_r12", [P, NT])
        u = sb("u", [P, NT, P])
        nn = sb("nn", [P, NT, P])
        nT = sb("nT", [P, TOK])
        dtx = sb("dtx", [P, NT * MHEADS])
        dt_abs = sb("dt_absx", [P, NT * MHEADS])
        dt_exp = sb("dt_expx", [P, NT * MHEADS])
        dt_s = sb("dt_s", [P, NT * MHEADS])
        dt_s2 = sb("dt_s2", [P, NT * MHEADS])
        dt_poly = sb("dt_poly", [P, NT * MHEADS])
        dta = sb("dta", [P, NT * MHEADS])
        dt = sb("dt", [P, NT * MHEADS])
        dA = sb("dA", [P, NT * MHEADS])
        pad = sb("pad", [P, 4, CONV - 1 + TOK])
        xbc = sb("xbc", [P, 4, TOK])
        zs = sb("zs", [P, 2, TOK])
        xdt = sb("xdt", [P, NT, INNER])
        bc = sb("bc", [P, TRI])
        Lall = sb("Lall", [P, 2 * TRI])
        L = [Lall[:, i * TRI:(i + 1) * TRI] for i in range(2)]

        def in_l(i):
            return Lall[:, i * TOK:(i + 1) * TOK].rearrange("p (t e) -> p t e", e=P)

        Mall = sb("Mall", [P, 2 * TRI])
        M = [Mall[:, i * TRI:(i + 1) * TRI] for i in range(2)]
        acc = [Mall[:, c * TOK:(c + 1) * TOK] for c in range(4)]
        gl = Mall[:, 0:4 * TOK].rearrange("p (f n) -> p f n", f=4)
        yd = sb("yd", [P, 2, TOK])
        yz = sb("yz", [P, 2, TOK])
        y2 = yd
        ss = sb("ss", [P, NT])
        rs = sb("rs", [P, NT])
        u2 = in_l(0)
        usq = in_l(1)
        ss2 = sb("ss2", [P, NT])
        r3_eps = sb("r3_eps", [P, NT])
        r3 = sb("r3", [P, NT])
        h3 = in_l(2)
        x2b = in_l(3)
        h3T = Lall[:, 4 * TOK:5 * TOK]
        x3 = x1b
        st4 = sb("st4", [P, NT, 6])
        d_mv = sb("d_mv", [P, NT, 2])
        d_veps = sb("d_veps", [P, NT])
        d_rstd = sb("d_rstd", [P, NT])
        n4 = n1
        x3b = nn
        n4T = n1T
        x4 = x2

        s = {n: ctx.enter_context(nc.semaphore(n)) for n in NAMES}
        nums = sorted(q.num for q in s.values())
        assert nums == list(range(nums[0], nums[0] + len(nums)))
        loop_sems = range(nums[0], nums[-1] + 1)
        misc_full = [s["misc_full0"], s["misc_full1"]]
        misc_free = [s["misc_free0"], s["misc_free1"]]

        loaded = ctx.enter_context(nc.semaphore("attention_weights_loaded"))
        tail_loaded = ctx.enter_context(nc.semaphore("tail_weights_loaded"))
        x0_loaded = ctx.enter_context(nc.semaphore("first_x_loaded"))
        su_pe = ctx.enter_context(nc.semaphore("setup_products"))
        su_act = ctx.enter_context(nc.semaphore("setup_act"))
        su_pool = ctx.enter_context(nc.semaphore("setup_pool"))

        attention_sync = [(wq_t, "wq_t"), (wk_t, "wk_t"), (wo[:], "wo"), (mask[:], "mask")]
        attention_act = [(bq[:], "bq"), (wv, "wv"), (bv[:], "bv"), (eye_row[:], "eye_row"), (row_out_b[:], "out_b")]
        tail_loads = [(ffn_wt, "ffn_wt"), (ffn_b, "ffn_b"), (up_t, "up_t"), (lora_up_t, "lora_up_t"),
                      (lora_down_t, "lora_down_t"), (down_aux, "down_aux"), (norm1, "norm1"), (norm2, "norm2"),
                      (win_t, "win_t"), (w1, "w1"), (w2, "w2"), (wmo, "wmo"), (conv_w, "conv_w"), (conv_b, "conv_b"),
                      (dt_bias, "dt_bias"), (a_log, "a_log"), (d_col, "d_col"), (mnorm, "mnorm"), (b1, "b1"), (b2, "b2")]
        ATTENTION_LOADED = 16 * (len(attention_sync) + len(attention_act))
        TAIL_LOADED = 16 * len(tail_loads)

        with nc.Block() as block:
            @block.sync
            def _(sp):
                for t, name in attention_sync[:2]:
                    sp.dma_start(t, a[name]).then_inc(loaded, 16)
                sp.dma_start(xin[:], a["x"][0].rearrange("(t p) e -> p t e", p=P)).then_inc(x0_loaded, 16)
                for t, name in attention_sync[2:]:
                    sp.dma_start(t, a[name]).then_inc(loaded, 16)
                for t, name in tail_loads:
                    sp.dma_start(t[:], a[name]).then_inc(tail_loaded, 16)

            @block.gpsimd
            def _(pool):
                nc.gpsimd.memset(ones[:], 1.0)
                nc.gpsimd.memset(neg_half[:], -0.5)
                nc.gpsimd.memset(neg_one[:], -1.0)
                nc.gpsimd.memset(pad[:], 0.0)
                pool.wait_ge(loaded, ATTENTION_LOADED)
                pool.wait_ge(su_act, 1)
                nc.gpsimd.tensor_tensor(wvl[:], wv, wvh[:].bitcast(F32), ALU.subtract).then_inc(su_pool, 1)
                pool.wait_ge(su_pool, 1)

            @block.tensor
            def _(pe):
                pe.wait_ge(loaded, ATTENTION_LOADED)
                for bank_of in range(2):
                    for odd in range(2):
                        ps = (psT if odd else psS)[bank_of]
                        for h in range(8 * bank_of + odd, 8 * bank_of + 8, 2):
                            half = slice(HD * odd, HD * odd + HD)
                            at = P * (h % 8 // 2)
                            last = nc.tensor.matmul(ps[:, at:at + P], wq_t[half, h // 2, :],
                                                    wk_t[half, h // 2, :], start=True, stop=True)
                        last.then_inc(su_pe, 1)
                for h in range(HEADS):
                    half = slice(HD * (h % 2), HD * (h % 2) + HD)
                    last = nc.tensor.matmul((psO if h % 2 else psG)[:, 256 + h:257 + h], wk_t[half, h // 2, :],
                                            bq[half, h // 2:h // 2 + 1], start=True, stop=True)
                for p in range(PAIRS):
                    last = nc.tensor.matmul(psO[:, 0:P], bv[:, p:p + 1].to_broadcast([P, P]), wo[:, p, :],
                                            start=(p == 0), stop=(p == PAIRS - 1))
                last.then_inc(su_pe, 1)

            four = [(slice(8 * k + odd, 8 * k + odd + 7, 2), (psT if odd else psS)[k]) for k in range(2) for odd in range(2)]

            @block.scalar
            def _(act):
                for t, name in attention_act:
                    act.dma_start(t, a[name]).then_inc(loaded, 16)
                act.wait_ge(loaded, ATTENTION_LOADED)
                nc.scalar.copy(wvh[:], wv).then_inc(su_act, 1)
                for n, (heads, ps) in enumerate(four):
                    act.wait_ge(su_pe, n + 1)
                    nc.scalar.copy(mh[:, heads, :], ps[:].rearrange("p (h e) -> p h e", e=P)).then_inc(su_act, 1)

            @block.vector
            def _(dve):
                dve.wait_ge(loaded, ATTENTION_LOADED)
                for n, (heads, ps) in enumerate(four):
                    dve.wait_ge(su_act, n + 2)
                    nc.vector.tensor_tensor(ml[:, heads, :], ps[:].rearrange("p (h e) -> p h e", e=P),
                                            mh[:, heads, :].bitcast(F32), ALU.subtract)
                dve.wait_ge(su_pe, 5)
                for odd, ps in enumerate((psG, psO)):
                    nc.vector.tensor_copy(cq[:, odd:HEADS:2], ps[:, 256 + odd:256 + HEADS:2])
                nc.vector.tensor_tensor(row_out_b[:], psO[:, 0:P], row_out_b[:], ALU.add)

        STEPS = HEADS + 3
        SLOTS = STEPS * NT
        PE_AT = {
            5: ["n1T"], 6: ["ffn1"], 11: ["nT"], 13: ["dt"], 15: ["xc0"], 16: ["xc1"],
            18: ["xc2", "xc3", "z0"], 22: ["z1"], 27: ["xdt0"], 29: ["xdt1"], 30: ["bc0"], 31: ["bc1"],
            32: ["bc2"], 33: ["da0"], 35: ["da1"], 39: ["da2"], 42: ["y0.0"], 43: ["y0.1"], 47: ["da3"],
            51: ["y1.0", "y1.1"], 53: ["ss"], 54: ["mo.0"], 55: ["mo.1"], 61: ["h3T"], 63: ["g0"],
            64: ["g1"], 65: ["g2"], 66: ["g3"], 68: ["nxT", "mlp.0"], 69: ["mlp.1", "gx"],
            72: ["n4T"], 74: ["ffn2"]}
        FOLD_AT = {8: ["lora1"], 10: ["lora2"], 12: ["lora3"]}
        FRONT_USES = ("nxT", "gx")
        AT = dict(
            stats1=0, rstd1=2, norm1=3, n1T=5, x2=7, r12=8, u=11, n=10, nT=11, dtx=13,
            pads=(16, 17, 18, 19), softplus=14, dt_exp=15, softplus_end=16,
            conv=(17, 17, 18, 18, 19, 19, 20, 20, 21, 21, 22, 22, 23, 23, 24, 24), tanh=(19, 22, 23, 25),
            silu=(20, 22, 26, 28), ztanh=(20, 21), zsilu=(21, 22), decay=24, xdt=(28, 29), bc=(31, 32, 33),
            scan=(33, 35, 37, 38, 41, 42, 48, 49), mul=(35, 36, 38, 39, 43, 46, 48, 49), y=(46, 51),
            ysq=(47, 50), ss=55, rs=55, u2=58, ssum=59, r3=59, h3=60, x2b=60, h3T=63, gelu=(64, 66), x3=69,
            rstd4=69, norm4=70, x3b=70, n4T=73, x4=75, front_stats=40, front_rstd=41, front_norm=44,
            front_h=68, front_split=68, front_g=69, front_gh=70, front_gl=70)
        G_AT = dict(project=0, copy=1, split=2, rest=2)
        V_AT = 1
        V_LATER = 0
        PAIR_AT = dict(invert=4, spread=7, turn_r=9, copy_r=9, attend=(9, 11, 13, 13), normalise=14)
        LAST_AT = dict(invert=4, spread=6, turn_r=8, copy_r=8, attend=(8, 8, 9, 9), normalise=10)
        PROJECT = 69
        ACT_TILES = 3

        def pair_slot(p, stage):
            return NT * (2 * p + 1) + (PAIR_AT if p < PAIRS - 1 else LAST_AT)[stage]

        def pairs_at(k, stage):
            return [p for p in range(PAIRS) if pair_slot(p, stage) == k]

        def attend_at(k):
            return [(p, j) for p in range(PAIRS) for j in range(NT)
                    if NT * (2 * p + 1) + (PAIR_AT if p < PAIRS - 1 else LAST_AT)["attend"][j] == k]

        def iteration(ia, it, nxt, block):
            att, tail, front = ia is not None, it is not None, nxt is not None
            fold = att and not tail
            uses = []
            for k in range(SLOTS):
                if att:
                    uses += [f"r{p}" for p in pairs_at(k, "turn_r")]
                if fold:
                    uses += FOLD_AT.get(k, [])
                uses += [n.split(".")[0] for n in PE_AT.get(k, [])
                         if (front if n in FRONT_USES else tail) and n[-2:] not in (".1", ".2", ".3")]
            order = {name: n for n, name in enumerate(uses)}

            def X(name):
                return psX[order[name] % 2]

            def fill(pe, name):
                n = order[name]
                if n >= 2:
                    pe.wait_ge(misc_free[n % 2], n // 2)
                return psX[n % 2]

            def full(name):
                return misc_full[order[name] % 2]

            def free(name):
                return misc_free[order[name] % 2]

            def count(name):
                return order[name] // 2 + 1

            def wait_full(eng, name):
                eng.wait_ge(full(name), count(name))
                return X(name)

            def wait_read(eng, name):
                eng.wait_ge(free(name), count(name))

            def wait_pt(eng, h, t):
                if t < ACT_TILES:
                    eng.wait_ge(s["pt_act"], ACT_TILES * h + t + 1)
                else:
                    eng.wait_ge(s["pt_dve"], (NT - ACT_TILES) * h + t - ACT_TILES + 1)

            @block.sync
            def _(sp):
                if front and att:
                    sp.wait_ge(s["xb_ready"], NT)
                    sp.dma_start(xin[:], a["x"][nxt].rearrange("(t p) e -> p t e", p=P)).then_inc(s["x_loaded"], 16)
                if tail:
                    wait_read(sp, "ffn2")
                    sp.dma_start(out[it].rearrange("(t p) e -> p t e", p=P), x4[:]).then_inc(s["out_dma"], 16)
                    sp.wait_ge(s["out_dma"], 16)

            def three_passes(ps, lhs, rhs):
                (lh, ll), (rh, rl) = lhs, rhs
                nc.tensor.matmul(ps, lh, rh, start=True, stop=False)
                nc.tensor.matmul(ps, lh, rl, start=False, stop=False)
                return nc.tensor.matmul(ps, ll, rh, start=False, stop=True)

            @block.tensor
            def _(pe):
                def project_g(h):
                    if h >= 2:
                        pe.wait_ge(s["g_evac"], h - 1)
                    three_passes(psG[:], (mh[:, h, :], ml[:, h, :]), (hTh[:], hTl[:])).then_inc(s["g_full"], 1)

                def project_v(n):
                    t, half = divmod(n, 2)
                    if n >= 1:
                        pe.wait_ge(s["v_evac"], n)
                    cols = slice(512 * half, 512 * half + 512)
                    three_passes(psO[:], (hTh[:, P * t:P * t + P], hTl[:, P * t:P * t + P]),
                                 (wvh[:, cols], wvl[:, cols])).then_inc(s["v_full"], 1)

                def scores(h, t):
                    n = NT * h + t
                    if n >= 2:
                        pe.wait_ge(s["sm_ready"], n - 1)
                    if t == 0 and h >= 1:
                        pe.wait_ge(s["gh_ready"], h)
                        pe.wait_ge(s["gl_ready"], h)
                    w = tile_cols(t)
                    q = slice(P * t, P * t + P)
                    three_passes(psS[n % 2][:, 0:w], (Gh[h % 2][:, q], Gl[h % 2][:, q]),
                                 (hTh[:, 0:w], hTl[:, 0:w])).then_inc(s["s_full"], 1)

                def turn(h, t):
                    n = NT * h + t
                    if n >= 2:
                        wait_pt(pe, (n - 2) // NT, (n - 2) % NT)
                    pe.wait_ge(s["p_ready"], n + 1)
                    for j in range(t + 1):
                        last = nc.tensor.transpose(psT[n % 2][:, P * j:P * j + P],
                                                   Pr[h % 2][:, TRI_AT[t] + P * j:TRI_AT[t] + P * j + P], ident)
                    last.then_inc(s["t_full"], 1)

                def turn_r(p):
                    ps = fill(pe, f"r{p}")
                    pe.wait_ge(s["spread_ready"], p + 1)
                    for t in range(NT):
                        last = nc.tensor.transpose(ps[:, P * t:P * t + P], R[:, P * t:P * t + P], ident)
                    last.then_inc(full(f"r{p}"), 1)

                def attend(p, j):
                    if j == 0:
                        wait_pt(pe, 2 * p + 1, ACT_TILES - 1)
                        wait_pt(pe, 2 * p + 1, NT - 1)
                        if p >= 1:
                            pe.wait_ge(s["o_ready"], p)
                        else:
                            pe.wait_ge(s["v_evac"], 2 * NT)
                    for hh in range(2):
                        h = 2 * p + hh
                        last = nc.tensor.matmul(psO[HD * hh:HD * hh + HD, P * j:TOK], V[:, j, HD * h:HD * h + HD],
                                                PT[h % 4][:, j, P * j:TOK], start=(j == 0), stop=(j == NT - 1),
                                                skip_group_check=True)
                    if j == NT - 1:
                        last.then_inc(s["pv_done"], 1)

                def project_out(first, last_pair):
                    pe.wait_ge(s["o_ready"], last_pair)
                    if first == 0:
                        pe.wait_ge(s["g_evac"], HEADS - 1)
                    for t in range(NT):
                        for p in range(first, last_pair):
                            last = nc.tensor.matmul(psG[:, P * t:P * t + P], V[:, t, P * p:P * p + P], wo[:, p, :],
                                                    start=(p == 0 and t == 0), stop=(p == PAIRS - 1),
                                                    skip_group_check=True)
                    last.then_inc(s["y_full"], 1)

                def transposed(name, src):
                    ps = fill(pe, name)
                    for t in range(NT):
                        last = nc.tensor.transpose(ps[:, P * t:P * t + P], src[:, t, :], ident)
                    last.then_inc(full(name), 1)

                def linear(name, lhsT, w):
                    ps = fill(pe, name)
                    for t in range(NT):
                        last = nc.tensor.matmul(ps[:, P * t:P * t + P], lhsT[:, P * t:P * t + P], w, start=True, stop=True)
                    last.then_inc(full(name), 1)

                def channels(name, w, x):
                    ps = fill(pe, name)
                    nc.tensor.matmul(ps[:], w, x, start=True, stop=True).then_inc(full(name), 1)

                def tail_use(name, part):
                    if name == "n1T":
                        pe.wait_ge(s["n1_ready"], NT)
                        transposed(name, n1)
                    elif name == "ffn1":
                        wait_read(pe, "n1T")
                        linear(name, n1T, ffn_wt[:])
                    elif name == "nT":
                        pe.wait_ge(s["n_ready"], NT)
                        transposed(name, nn)
                    elif name == "dt":
                        wait_read(pe, "nT")
                        ps = fill(pe, name)
                        for t in range(NT):
                            last = nc.tensor.matmul(ps[:, MHEADS * t:MHEADS * t + MHEADS], nT[:, P * t:P * t + P],
                                                    win_t[:, 768:772], start=True, stop=True)
                        last.then_inc(full(name), 1)
                    elif name[:2] == "xc":
                        c = int(name[2])
                        channels(name, win_t[:, INNER + P * c:INNER + P * c + P], nT[:])
                    elif name[0] == "z":
                        c = int(name[1])
                        channels(name, win_t[:, P * c:P * c + P], nT[:])
                    elif name[:3] == "xdt":
                        k = int(name[3])
                        pe.wait_ge(s["silu_ready"], 2)
                        ps = fill(pe, name)
                        for tt in range(2):
                            for c in range(2):
                                t = 2 * k + tt
                                last = nc.tensor.transpose(ps[:, INNER * tt + P * c:INNER * tt + P * c + P],
                                                           xbc[:, c, P * t:P * t + P], ident)
                        last.then_inc(full(name), 1)
                    elif name[:2] == "bc":
                        pe.wait_ge(s["silu_ready"], 4)
                        ps = fill(pe, name)
                        at = 0
                        for j in BC_TILES[int(name[2])]:
                            w = TOK - P * j
                            last = nc.tensor.matmul(ps[:, at:at + w], xbc[:, 2, P * j:P * j + P], xbc[:, 3, P * j:TOK],
                                                    start=True, stop=True)
                            at += w
                        last.then_inc(full(name), 1)
                    elif name[:2] == "da":
                        pe.wait_ge(s["da_ready"], 1)
                        ps = fill(pe, name)
                        for t in range(NT):
                            k = MHEADS * t + int(name[2])
                            last = nc.tensor.transpose(ps[:, P * t:P * t + P], dA[:, k:k + 1].to_broadcast([P, P]), ident)
                        last.then_inc(full(name), 1)
                    elif name in ("y0", "y1"):
                        p = int(name[1])
                        if part == 0:
                            fill(pe, name)
                            for k in range(2):
                                wait_read(pe, f"xdt{k}")
                            pe.wait_ge(s["m_ready"], 4 * p + 4)
                        ps = X(name)
                        for j in (0,) if part == 0 else (1, 2, 3):
                            for hh in range(2):
                                h = 2 * p + hh
                                last = nc.tensor.matmul(ps[HD * hh:HD * hh + HD, P * j:TOK], xdt[:, j, HD * h:HD * h + HD],
                                                        M[h % 2][:, COL_AT[j]:COL_AT[j] + TOK - P * j], start=(j == 0),
                                                        stop=(j == NT - 1), skip_group_check=True)
                        if part == 1:
                            last.then_inc(full(name), 1)
                    elif name == "ss":
                        ps = fill(pe, name)
                        pe.wait_ge(s["y2_ready"], 2)
                        for t in range(NT):
                            for c in range(2):
                                last = nc.tensor.matmul(ps[:, t:t + 1], y2[:, c, P * t:P * t + P], ones[:],
                                                        start=(c == 0), stop=(c == 1), skip_group_check=True)
                        last.then_inc(full(name), 1)
                    elif name == "mo":
                        ps = X(name)
                        if part == 0:
                            fill(pe, name)
                            pe.wait_ge(s["yz_ready"], 2)
                        for t in (2 * part, 2 * part + 1):
                            for c in range(2):
                                last = nc.tensor.matmul(ps[:, P * t:P * t + P], yz[:, c, P * t:P * t + P], wmo[:, c, :],
                                                        start=(c == 0), stop=(c == 1), skip_group_check=True)
                        if part == 1:
                            last.then_inc(full(name), 1)
                    elif name == "h3T":
                        pe.wait_ge(s["h3_ready"], NT)
                        transposed(name, h3)
                    elif name in ("g0", "g1", "g2", "g3"):
                        f = int(name[1])
                        wait_read(pe, "h3T")
                        channels(name, w1[:, P * f:P * f + P], h3T)
                    elif name == "mlp":
                        ps = X(name)
                        if part == 0:
                            fill(pe, name)
                            for f in range(4):
                                wait_read(pe, f"g{f}")
                        for t in (2 * part, 2 * part + 1):
                            for f in range(4):
                                last = nc.tensor.matmul(ps[:, P * t:P * t + P], gl[:, f, P * t:P * t + P], w2[:, f, :],
                                                        start=(f == 0), stop=(f == 3), skip_group_check=True)
                        if part == 1:
                            last.then_inc(full(name), 1)
                    elif name == "n4T":
                        pe.wait_ge(s["n4_ready"], NT)
                        transposed(name, n4)
                    elif name == "ffn2":
                        wait_read(pe, "n4T")
                        linear(name, n4T, ffn_wt[:])

                def front_use(name):
                    if name == "nxT":
                        pe.wait_ge(s["xn_ready"], NT)
                        transposed(name, xn)
                    elif name == "gx":
                        pe.wait_ge(s["hTh_ready"], 1)
                        pe.wait_ge(s["hTl_ready"], 1)
                        ps = fill(pe, name)
                        three_passes(ps[:], (mh[:, 0, :], ml[:, 0, :]), (hTh[:], hTl[:])).then_inc(full(name), 1)

                def fold_use(name):
                    ps = fill(pe, name)
                    if name == "lora1":
                        pe.wait_ge(tail_loaded, TAIL_LOADED)
                        last = nc.tensor.matmul(ps[0:4, 0:P], lora_down_t[:], down_aux[:], start=True, stop=True)
                    elif name == "lora2":
                        wait_read(pe, "lora1")
                        last = nc.tensor.matmul(ps[0:50, 0:P], lora_up_t[:], lora1[:], start=True, stop=True)
                    else:
                        wait_read(pe, "lora2")
                        last = nc.tensor.matmul(ps[:, 0:P], lora2[:], up_t[:], start=True, stop=True)
                    last.then_inc(full(name), 1)

                for k in range(SLOTS):
                    step, t = divmod(k, NT)
                    if fold:
                        for name in FOLD_AT.get(k, []):
                            fold_use(name)
                    if att:
                        if step < HEADS:
                            scores(step, t)
                        if 1 <= step <= HEADS:
                            turn(step - 1, t)
                        if 0 <= k - V_AT < 2 * NT:
                            project_v(k - V_AT)
                        for p in pairs_at(k, "turn_r"):
                            turn_r(p)
                        if t == G_AT["project"] and step + 1 < HEADS:
                            project_g(step + 1)
                        for p, j in attend_at(k):
                            attend(p, j)
                        if k == PROJECT:
                            project_out(0, PAIRS - 1)
                    for name in PE_AT.get(k, []):
                        if name in FRONT_USES:
                            if front:
                                front_use(name)
                        elif tail:
                            base, _, part = name.partition(".")
                            tail_use(base, int(part or 0))
                if att:
                    project_out(PAIRS - 1, PAIRS)

            @block.scalar
            def _(act):
                def copy_g(h):
                    act.wait_ge(s["g_full"], h)
                    if h >= 2:
                        act.wait_ge(s["gh_ready"], h - 1)
                        act.wait_ge(s["gl_ready"], h - 1)
                    nc.scalar.activation(G[:], psG[:], ACT.Identity, bias=cq[:, h:h + 1]).then_inc(s["g_evac"], 1)

                def copy_v(n):
                    act.wait_ge(s["v_full"], n + 1)
                    nc.scalar.copy(V[:, n // 2, 0:512], psO[:]).then_inc(s["v_evac"], 1)

                def probs(h, t):
                    n = NT * h + t
                    act.wait_ge(s["sm_ready"], n + 1)
                    if h >= 2:
                        act.wait_ge(s["t_full"], n - 2 * NT + 1)
                    w = tile_cols(t)
                    nc.scalar.activation(Pr[h % 2][:, TRI_AT[t]:TRI_AT[t] + w], Sm[n % 3][:, 0:w], ACT.Exp,
                                         bias=nb[:, n:n + 1], scale=-1.0,
                                         accum_out=den[:, h, t:t + 1]).then_inc(s["p_ready"], 1)

                def copy_t(h, t):
                    act.wait_ge(s["t_full"], NT * h + t + 1)
                    if h >= 4:
                        act.wait_ge(s["pv_done"], (h - 4) // 2 + 1)
                    src = psT[(NT * h + t) % 2][:, 0:tile_cols(t)].rearrange("p (j q) -> p j q", q=P)
                    nc.scalar.copy(PT[h % 4][:, 0:t + 1, P * t:P * t + P], src).then_inc(s["pt_act"], 1)

                def copy_r(p):
                    evacuate(R[:], f"r{p}")

                def evacuate(dst, name):
                    ps = wait_full(act, name)
                    nc.scalar.copy(dst, ps[:]).then_inc(free(name), 1)

                def tail_part(k):
                    if k == AT["n1T"]:
                        evacuate(n1T[:], "n1T")
                    if k == AT["nT"]:
                        evacuate(nT[:], "nT")
                    if k in AT["pads"]:
                        c = AT["pads"].index(k)
                        evacuate(pad[:, c, CONV - 1:], f"xc{c}")
                    if k == AT["dt_exp"]:
                        act.wait_ge(s["dt_abs"], 1)
                        nc.scalar.activation(dt_exp[:], dt_abs[:], ACT.Exp, scale=-1.0).then_inc(s["dt_exp"], 1)
                    if k in AT["tanh"]:
                        c = AT["tanh"].index(k)
                        act.wait_ge(s["conv_ready"], c + 1)
                        nc.scalar.activation(xbc[:, c, :], acc[c], ACT.Tanh).then_inc(s["tanh_ready"], 1)
                    if k in AT["ztanh"]:
                        c = AT["ztanh"].index(k)
                        ps = wait_full(act, f"z{c}")
                        nc.scalar.activation(zs[:, c, :], ps[:], ACT.Tanh).then_inc(s["ztanh_ready"], 1)
                    if k == AT["decay"]:
                        act.wait_ge(s["dta_ready"], 1)
                        nc.scalar.activation(dA[:], dta[:], ACT.Exp, scale=-1.0).then_inc(s["da_ready"], 1)
                    if k in AT["bc"]:
                        n = AT["bc"].index(k)
                        ps = wait_full(act, f"bc{n}")
                        at = 0
                        for j in BC_TILES[n]:
                            w = TOK - P * j
                            last = nc.scalar.copy(bc[:, COL_AT[j]:COL_AT[j] + w], ps[:, at:at + w])
                            at += w
                        last.then_inc(free(f"bc{n}"), 1)
                    if k in AT["ysq"]:
                        c = AT["ysq"].index(k)
                        act.wait_ge(s["yz_ready"], c + 1)
                        nc.scalar.activation(y2[:, c, :], yz[:, c, :], ACT.Square).then_inc(s["y2_ready"], 1)
                    if k == AT["ssum"]:
                        wait_read(act, "mo")
                        for t in range(NT):
                            nc.scalar.activation(usq[:, t, :], u2[:, t, :], ACT.Square,
                                                 accum_out=ss2[:, t:t + 1]).then_inc(s["ss2_ready"], 1)
                    if k == AT["h3T"]:
                        evacuate(h3T, "h3T")
                    if k in AT["gelu"]:
                        for f in (0, 1) if k == AT["gelu"][0] else (2, 3):
                            ps = wait_full(act, f"g{f}")
                            nc.scalar.activation(gl[:, f, :], ps[:], ACT.Gelu, bias=b1[:, f:f + 1]).then_inc(free(f"g{f}"), 1)
                    if k == AT["n4T"]:
                        evacuate(n4T[:], "n4T")

                def front_part(k):
                    if k == AT["front_h"]:
                        evacuate(hT, "nxT")
                    if k == AT["front_g"]:
                        ps = wait_full(act, "gx")
                        if att:
                            act.wait_ge(s["gh_ready"], HEADS - 1)
                            act.wait_ge(s["gl_ready"], HEADS - 1)
                        nc.scalar.activation(G[:], ps[:], ACT.Identity, bias=cq[:, 0:1]).then_inc(free("gx"), 1)

                def fold_part(k):
                    if "lora1" in FOLD_AT.get(k, []):
                        ps = wait_full(act, "lora1")
                        nc.scalar.copy(lora1[:], ps[0:4, 0:P]).then_inc(free("lora1"), 1)
                        act.wait_ge(tail_loaded, TAIL_LOADED)
                        nc.scalar.activation(exp_a[:], a_log[:], ACT.Exp)
                    if "lora2" in FOLD_AT.get(k, []):
                        ps = wait_full(act, "lora2")
                        nc.scalar.copy(lora2[:], ps[0:50, 0:P]).then_inc(free("lora2"), 1)

                for k in range(SLOTS):
                    step, t = divmod(k, NT)
                    if fold:
                        fold_part(k)
                    if att:
                        if step < HEADS:
                            probs(step, t)
                        if 0 <= k - V_AT - V_LATER < 2 * NT and (k - V_AT - V_LATER) % 2 == 0:
                            copy_v(k - V_AT - V_LATER)
                        for p in pairs_at(k, "copy_r"):
                            copy_r(p)
                        if t < ACT_TILES and 1 <= step <= HEADS:
                            copy_t(step - 1, t)
                        if t == G_AT["copy"] and step + 1 < HEADS:
                            copy_g(step + 1)
                    if tail:
                        tail_part(k)
                    if front:
                        front_part(k)

            @block.vector
            def _(dve):
                chained = [0]

                def chain(last):
                    chained[0] += 1
                    last.then_inc(s["dve_chain"], 1)
                    dve.wait_ge(s["dve_chain"], chained[0])

                def flat(x):
                    return x[:, :, :].rearrange("p t e -> p (t e)")

                def statistics(x, stats, mv, ready):
                    for t in range(NT):
                        last = nc.vector.bn_stats(stats[:, t, :], x[:, t, :])
                    chain(last)
                    for t in range(NT):
                        last = nc.vector.bn_aggr(mv[:, t, :], stats[:, t, :])
                    last.then_inc(ready, 1)

                def normalise(dst, x, mv, rstd, ready):
                    for t in range(NT):
                        nc.vector.tensor_scalar(dst[:, t, :], x[:, t, :], mv[:, t, 0:1], rstd[:, t:t + 1],
                                                ALU.subtract, ALU.mult).then_inc(ready, 1)

                def copy_v(n):
                    dve.wait_ge(s["v_full"], n + 1)
                    nc.vector.tensor_copy(V[:, n // 2, 512:1024], psO[:]).then_inc(s["v_evac"], 1)

                def split_g(h):
                    dve.wait_ge(s["g_evac"], h)
                    if h >= 2:
                        dve.wait_ge(s["s_full"], NT * (h - 1))
                    if h >= 3:
                        dve.wait_ge(s["gl_ready"], h - 2)
                    nc.vector.tensor_copy(Gh[h % 2][:], G[:]).then_inc(s["gh_ready"], 1)

                def mask_and_max(h, t):
                    n = NT * h + t
                    dve.wait_ge(s["s_full"], n + 1)
                    if n >= 3:
                        dve.wait_ge(s["p_ready"], n - 2)
                    w = tile_cols(t)
                    nc.vector.tensor_tensor_reduce(
                        out=Sm[n % 3][:, 0:w], in0=psS[n % 2][:, 0:w], in1=mask[:, TOK - w:TOK], scale=-SCALE,
                        scalar=3.0e38, op0=ALU.add, op1=ALU.min, accum_out=nb[:, n:n + 1]).then_inc(s["sm_ready"], 1)

                def copy_t(h, t):
                    dve.wait_ge(s["t_full"], NT * h + t + 1)
                    if h >= 4:
                        dve.wait_ge(s["pv_done"], (h - 4) // 2 + 1)
                    src = psT[(NT * h + t) % 2][:, 0:tile_cols(t)].rearrange("p (j q) -> p j q", q=P)
                    nc.vector.tensor_copy(PT[h % 4][:, 0:t + 1, P * t:P * t + P], src).then_inc(s["pt_dve"], 1)

                def invert(p):
                    dve.wait_ge(s["p_ready"], NT * (2 * p + 2))
                    nc.vector.reciprocal(rden[:, 2 * p:2 * p + 2, :], den[:, 2 * p:2 * p + 2, :]).then_inc(s["rden_ready"], 1)

                def normalise_o(p):
                    dve.wait_ge(s["pv_done"], p + 1)
                    wait_read(dve, f"r{p}")
                    nc.vector.tensor_tensor(V[:, :, P * p:P * p + P], psO[:].rearrange("p (t q) -> p t q", q=P),
                                            R[:].rearrange("p (t q) -> p t q", q=P), ALU.mult).then_inc(s["o_ready"], 1)

                def end():
                    dve.wait_ge(s["y_full"], 2)
                    dve.wait_ge(s["xb_ready"], NT)
                    if tail:
                        dve.wait_ge(s["n1_ready"], NT)
                        dve.wait_ge(s["x1b_ready"], NT)
                    nc.vector.tensor_tensor(flat(x1), psG[:], flat(xb), ALU.add).then_inc(s["x1_ready"], 1)
                    dve.wait_ge(s["x1_ready"], 1)

                def add_to(dst, name, x, ready, n):
                    ps = wait_full(dve, name)
                    dve.wait_ge(ready, n)
                    nc.vector.tensor_tensor(flat(dst), ps[:], flat(x), ALU.add).then_inc(free(name), 1)
                    wait_read(dve, name)

                def convolve(c, tap):
                    if tap == CONV - 1:
                        wait_read(dve, f"xc{c}")
                        chain(nc.vector.tensor_scalar(acc[c], pad[:, c, tap:tap + TOK], conv_w[:, c, tap:tap + 1],
                                                      conv_b[:, c:c + 1], ALU.mult, ALU.add))
                        return
                    last = nc.vector.scalar_tensor_tensor(
                        out=acc[c], in0=pad[:, c, tap:tap + TOK], scalar=conv_w[:, c, tap:tap + 1], in1=acc[c],
                        op0=ALU.mult, op1=ALU.add)
                    if tap < CONV - 2:
                        chain(last)
                    else:
                        last.then_inc(s["conv_ready"], 1)

                def scan(h, js):
                    ps = wait_full(dve, f"da{h}")
                    if h >= 2:
                        dve.wait_ge(s["m_ready"], 2 * h - 2)
                    for j in js:
                        w = TOK - P * j
                        last = nc.vector.tensor_tensor_scan(L[h % 2][:, COL_AT[j]:COL_AT[j] + w], ps[:, P * j:TOK],
                                                            eye_row[:, 0:w], 0.0, ALU.mult, ALU.add)
                    if NT - 1 in js:
                        last.then_inc(free(f"da{h}"), 1)

                def tail_part(k):
                    if k == AT["stats1"]:
                        statistics(x1, st, a_mv, s["a_mv"])
                    if k == AT["norm1"]:
                        dve.wait_ge(s["a_mv"], 1)
                        dve.wait_ge(s["a_rstd"], 1)
                        normalise(n1, x1, a_mv, a_rstd, s["n1_ready"])
                    if k == AT["x2"]:
                        add_to(x2, "ffn1", x1b, s["x1b_ready"], NT)
                        statistics(x2, st2, b_mv, s["b_mv"])
                    if k == AT["u"]:
                        dve.wait_ge(s["b_mv"], 1)
                        dve.wait_ge(s["b_r12"], 1)
                        for t in range(NT):
                            nc.vector.tensor_scalar(u[:, t, :], x2[:, t, :], b_mv[:, t, 0:1], b_r1[:, t:t + 1],
                                                    ALU.subtract, ALU.mult)
                    if k == AT["n"]:
                        dve.wait_ge(s["b_mv"], 1)
                        dve.wait_ge(s["b_r12"], 1)
                        normalise(nn, x2, b_mv, b_r12, s["n_ready"])
                    if k == AT["dtx"]:
                        ps = wait_full(dve, "dt")
                        nc.vector.tensor_tensor(dtx[:], ps[:, 0:NT * MHEADS], dt_bias[:], ALU.add).then_inc(free("dt"), 1)
                    for n, at in enumerate(AT["conv"]):
                        if at == k:
                            convolve(n // CONV, (CONV - 1, 0, 1, 2)[n % CONV])
                    if k in AT["silu"]:
                        c = AT["silu"].index(k)
                        dve.wait_ge(s["tanh_ready"], c + 1)
                        nc.vector.scalar_tensor_tensor(out=xbc[:, c, :], in0=xbc[:, c, :], scalar=1.0, in1=acc[c],
                                                       op0=ALU.add, op1=ALU.mult).then_inc(s["silu_ready"], 1)
                    if k in AT["zsilu"]:
                        c = AT["zsilu"].index(k)
                        dve.wait_ge(s["ztanh_ready"], c + 1)
                        ps = wait_full(dve, f"z{c}")
                        nc.vector.scalar_tensor_tensor(out=zs[:, c, :], in0=zs[:, c, :], scalar=1.0, in1=ps[:],
                                                       op0=ALU.add, op1=ALU.mult).then_inc(free(f"z{c}"), 1)
                    if k in AT["xdt"]:
                        n = AT["xdt"].index(k)
                        dve.wait_ge(s["dt_ready"], 1)
                        ps = wait_full(dve, f"xdt{n}")
                        nc.vector.tensor_tensor(
                            xdt[:, 2 * n:2 * n + 2, :].rearrange("p t (h d) -> p (t h) d", d=HD),
                            ps[:].rearrange("p (g d) -> p g d", d=HD),
                            dt[:, 8 * n:8 * n + 8].unsqueeze(2).to_broadcast([P, 8, HD]),
                            ALU.mult).then_inc(free(f"xdt{n}"), 1)
                    if k in AT["scan"]:
                        h, part = divmod(AT["scan"].index(k), 2)
                        scan(h, (1, 2, 3) if part else (0,))
                    if k in AT["y"]:
                        c = AT["y"].index(k)
                        ps = wait_full(dve, f"y{c}")
                        dve.wait_ge(s["silu_ready"], c + 1)
                        nc.vector.scalar_tensor_tensor(out=yd[:, c, :], in0=xbc[:, c, :], scalar=d_col[:, c:c + 1],
                                                       in1=ps[:], op0=ALU.mult, op1=ALU.add).then_inc(free(f"y{c}"), 1)
                        wait_read(dve, f"y{c}")
                        wait_read(dve, f"z{c}")
                        nc.vector.tensor_tensor(yz[:, c, :], yd[:, c, :], zs[:, c, :], ALU.mult).then_inc(s["yz_ready"], 1)
                    if k == AT["ss"]:
                        ps = wait_full(dve, "ss")
                        nc.vector.tensor_scalar(ss[:], ps[:, 0:NT], 1.0 / INNER, LN_EPS, ALU.mult,
                                                ALU.add).then_inc(free("ss"), 1)
                    if k == AT["u2"]:
                        dve.wait_ge(s["rs_ready"], 1)
                        ps = wait_full(dve, "mo")
                        for t in range(NT):
                            last = nc.vector.scalar_tensor_tensor(
                                out=u2[:, t, :], in0=ps[:, P * t:P * t + P], scalar=rs[:, t:t + 1], in1=u[:, t, :],
                                op0=ALU.mult, op1=ALU.add)
                        last.then_inc(free("mo"), 1)
                    if k == AT["h3"]:
                        wait_read(dve, "mo")
                        dve.wait_ge(s["r3_ready"], 1)
                        for t in range(NT):
                            nc.vector.tensor_scalar(h3[:, t, :], u2[:, t, :], r3[:, t:t + 1], None,
                                                    ALU.mult).then_inc(s["h3_ready"], 1)
                    if k == AT["x3"]:
                        add_to(x3, "mlp", x2b, s["x2b_ready"], 1)
                        statistics(x3, st4, d_mv, s["d_mv"])
                    if k == AT["norm4"]:
                        dve.wait_ge(s["d_mv"], 1)
                        dve.wait_ge(s["d_rstd"], 1)
                        normalise(n4, x3, d_mv, d_rstd, s["n4_ready"])
                    if k == AT["x4"]:
                        add_to(x4, "ffn2", x3b, s["x3b_ready"], NT)

                def front_part(k):
                    if k == AT["front_stats"]:
                        dve.wait_ge(s["x_loaded"] if att else x0_loaded, 16)
                        statistics(xin, x_st, x_mv, s["x_mv"])
                    if k == AT["front_norm"]:
                        dve.wait_ge(s["x_mv"], 1)
                        dve.wait_ge(s["x_rstd"], 1)
                        normalise(xn, xin, x_mv, x_rstd, s["xn_ready"])
                    if k == AT["front_split"]:
                        wait_read(dve, "nxT")
                        if att:
                            dve.wait_ge(s["s_full"], NT * HEADS)
                        nc.vector.tensor_copy(hTh[:], hT).then_inc(s["hTh_ready"], 1)
                        dve.wait_ge(s["hTh_ready"], 1)
                        nc.vector.tensor_tensor(hTl[:], hT, hTh[:].bitcast(F32), ALU.subtract).then_inc(s["hTl_ready"], 1)
                    if k == AT["front_gh"]:
                        wait_read(dve, "gx")
                        nc.vector.tensor_copy(Gh[0][:], G[:]).then_inc(s["front_gh"], 1)

                def fold_part(k):
                    if "lora3" in FOLD_AT.get(k, []):
                        dve.wait_ge(tail_loaded, TAIL_LOADED)
                        ps = wait_full(dve, "lora3")
                        nc.vector.tensor_tensor(ffn_wt[:], ps[:, 0:P], ffn_wt[:], ALU.add).then_inc(free("lora3"), 1)
                        nc.vector.tensor_scalar(win_t[:, INNER:], win_t[:, INNER:], norm1[:, 0:1], None, ALU.mult)
                        nc.vector.tensor_scalar(win_t[:, 0:INNER], win_t[:, 0:INNER], norm1[:, 0:1], 0.5, ALU.mult, ALU.mult)
                        nc.vector.tensor_scalar(conv_w[:], conv_w[:], 0.5, None, ALU.mult)
                        nc.vector.tensor_scalar(conv_b[:], conv_b[:], 0.5, None, ALU.mult)
                        nc.vector.tensor_scalar(w1[:], w1[:], norm2[:, 0:1], None, ALU.mult)
                        for k in range(2):
                            nc.vector.tensor_scalar(wmo[:, k, :], wmo[:, k, :], mnorm[:, k:k + 1], None, ALU.mult)

                for k in range(SLOTS):
                    step, t = divmod(k, NT)
                    if fold:
                        fold_part(k)
                    if att:
                        for p in pairs_at(k, "invert"):
                            invert(p)
                        if step < HEADS:
                            mask_and_max(step, t)
                        if 0 <= k - V_AT - V_LATER < 2 * NT and (k - V_AT - V_LATER) % 2 == 1:
                            copy_v(k - V_AT - V_LATER)
                        if t >= ACT_TILES and 1 <= step <= HEADS:
                            copy_t(step - 1, t)
                        if t == G_AT["split"] and step + 1 < HEADS:
                            split_g(step + 1)
                        for p in pairs_at(k, "normalise"):
                            normalise_o(p)
                    if tail:
                        tail_part(k)
                    if front:
                        front_part(k)
                if att:
                    end()

            @block.gpsimd
            def _(pool):
                chained = [0]

                def chain(last):
                    chained[0] += 1
                    last.then_inc(s["pool_chain"], 1)
                    pool.wait_ge(s["pool_chain"], chained[0])

                def inverse_deviation(mv, veps, rstd, mv_ready, ready):
                    pool.wait_ge(mv_ready, 1)
                    chain(nc.gpsimd.tensor_scalar(veps[:], mv[:, :, 1], LN_EPS, None, ALU.add))
                    nc.gpsimd.tensor_tensor(rstd[:], veps[:], neg_half[:], ALU.pow).then_inc(ready, 1)

                def add_rows(dst, x, row, ready):
                    for t in range(NT):
                        nc.gpsimd.tensor_tensor(dst[:, t, :], x[:, t, :], row[:], ALU.add).then_inc(ready, 1)

                def split_g(h):
                    pool.wait_ge(s["gh_ready"], h)
                    if h >= 2:
                        pool.wait_ge(s["s_full"], NT * (h - 1))
                    nc.gpsimd.tensor_tensor(Gl[h % 2][:], G[:], Gh[h % 2][:].bitcast(F32),
                                            ALU.subtract).then_inc(s["gl_ready"], 1)

                def spread(p):
                    pool.wait_ge(s["rden_ready"], p + 1)
                    if p >= 1:
                        pool.wait_ge(s["o_ready"], p)
                    for t in range(NT):
                        last = nc.gpsimd.tensor_copy(R[:, P * t:P * t + P].rearrange("p (h d) -> p h d", d=HD),
                                                     rden[:, 2 * p:2 * p + 2, t:t + 1].to_broadcast([P, 2, HD]))
                    last.then_inc(s["spread_ready"], 1)

                def tail_part(k):
                    if k == AT["rstd1"]:
                        inverse_deviation(a_mv, a_veps, a_rstd, s["a_mv"], s["a_rstd"])
                        add_rows(x1b, x1, ffn_b, s["x1b_ready"])
                    if k == AT["r12"]:
                        pool.wait_ge(s["b_mv"], 1)
                        chain(nc.gpsimd.tensor_scalar(b_veps[:], b_mv[:, :, 1], LN_EPS, None, ALU.add))
                        chain(nc.gpsimd.tensor_tensor(b_r1[:], b_veps[:], neg_half[:], ALU.pow))
                        chain(nc.gpsimd.tensor_tensor(b_sq[:], b_r1[:], b_r1[:], ALU.mult))
                        chain(nc.gpsimd.tensor_tensor(b_sq[:], b_sq[:], b_mv[:, :, 1], ALU.mult))
                        chain(nc.gpsimd.tensor_scalar(b_sq[:], b_sq[:], float(P), BN_EPS, ALU.mult, ALU.add))
                        chain(nc.gpsimd.tensor_tensor(b_r2[:], b_sq[:], neg_half[:], ALU.pow))
                        nc.gpsimd.tensor_tensor(b_r12[:], b_r1[:], b_r2[:], ALU.mult).then_inc(s["b_r12"], 1)
                    if k == AT["softplus"]:
                        wait_read(pool, "dt")
                        chain(nc.gpsimd.tensor_scalar(dt_s[:], dtx[:], 0.0, 2.0, ALU.max, ALU.mult))
                        nc.gpsimd.tensor_tensor(dt_abs[:], dt_s[:], dtx[:], ALU.subtract).then_inc(s["dt_abs"], 1)
                    if k == AT["softplus_end"]:
                        pool.wait_ge(s["dt_exp"], 1)
                        chain(nc.gpsimd.tensor_scalar(dt_s[:], dt_exp[:], 2.0, None, ALU.add))
                        chain(nc.gpsimd.tensor_tensor(dt_s2[:], dt_s[:], neg_one[:], ALU.pow))
                        chain(nc.gpsimd.tensor_tensor(dt_s[:], dt_exp[:], dt_s2[:], ALU.mult))
                        chain(nc.gpsimd.tensor_tensor(dt_s2[:], dt_s[:], dt_s[:], ALU.mult))
                        coef = [2.0 / (2 * k + 1) for k in range(LOG_TERMS)]
                        chain(nc.gpsimd.tensor_scalar(dt_poly[:], dt_s2[:], coef[-1], coef[-2], ALU.mult, ALU.add))
                        for c in coef[LOG_TERMS - 3::-1]:
                            chain(nc.gpsimd.tensor_tensor(dt_poly[:], dt_poly[:], dt_s2[:], ALU.mult))
                            chain(nc.gpsimd.tensor_scalar(dt_poly[:], dt_poly[:], c, None, ALU.add))
                        chain(nc.gpsimd.tensor_tensor(dt_poly[:], dt_poly[:], dt_s[:], ALU.mult))
                        chain(nc.gpsimd.tensor_scalar(dt_s[:], dtx[:], 0.0, None, ALU.max))
                        nc.gpsimd.tensor_tensor(dt[:], dt_s[:], dt_poly[:], ALU.add).then_inc(s["dt_ready"], 1)
                        pool.wait_ge(s["dt_ready"], 1)
                        nc.gpsimd.tensor_tensor(dta[:], dt[:], exp_a[:], ALU.mult).then_inc(s["dta_ready"], 1)
                    if k in AT["mul"]:
                        h, part = divmod(AT["mul"].index(k), 2)
                        if part == 0:
                            for n in range(len(BC_TILES)):
                                wait_read(pool, f"bc{n}")
                            wait_read(pool, f"da{h}")
                            if h >= 2:
                                pool.wait_ge(full("y0"), count("y0"))
                        cols = slice(TRI // 2 * part, TRI // 2 * (part + 1))
                        nc.gpsimd.tensor_tensor(M[h % 2][:, cols], L[h % 2][:, cols], bc[:, cols],
                                                ALU.mult).then_inc(s["m_ready"], 1)
                    if k == AT["rs"]:
                        wait_read(pool, "ss")
                        nc.gpsimd.tensor_tensor(rs[:], ss[:], neg_half[:], ALU.pow).then_inc(s["rs_ready"], 1)
                    if k == AT["r3"]:
                        pool.wait_ge(s["ss2_ready"], NT)
                        chain(nc.gpsimd.tensor_scalar(r3_eps[:], ss2[:], BN_EPS, None, ALU.add))
                        nc.gpsimd.tensor_tensor(r3[:], r3_eps[:], neg_half[:], ALU.pow).then_inc(s["r3_ready"], 1)
                    if k == AT["x2b"]:
                        for t in range(NT):
                            last = nc.gpsimd.tensor_tensor(x2b[:, t, :], x2[:, t, :], u2[:, t, :], ALU.add)
                        chain(last)
                        for t in range(NT):
                            last = nc.gpsimd.tensor_tensor(x2b[:, t, :], x2b[:, t, :], b2[:], ALU.add)
                        last.then_inc(s["x2b_ready"], 1)
                    if k == AT["rstd4"]:
                        inverse_deviation(d_mv, d_veps, d_rstd, s["d_mv"], s["d_rstd"])
                    if k == AT["x3b"]:
                        add_rows(x3b, x3, ffn_b, s["x3b_ready"])

                def front_part(k):
                    if k == AT["front_rstd"]:
                        inverse_deviation(x_mv, x_veps, x_rstd, s["x_mv"], s["x_rstd"])
                    if k == AT["front_gl"]:
                        pool.wait_ge(s["front_gh"], 1)
                        nc.gpsimd.tensor_tensor(Gl[0][:], G[:], Gh[0][:].bitcast(F32), ALU.subtract).then_inc(s["front_gl"], 1)
                        pool.wait_ge(s["front_gl"], 1)

                if att:
                    add_rows(xb, xin, row_out_b, s["xb_ready"])
                for k in range(SLOTS):
                    step, t = divmod(k, NT)
                    if att:
                        if t == G_AT["rest"] and step + 1 < HEADS:
                            split_g(step + 1)
                        for p in pairs_at(k, "spread"):
                            spread(p)
                    if tail:
                        tail_part(k)
                    if front:
                        front_part(k)

        batch = a["x"].shape[0]
        with nc.Block() as block:
            iteration(None, None, 0, block)
        nc.all_engine_barrier(sems_to_clear=loop_sems)
        with nc.Block() as block:
            iteration(0, None, 1, block)
        nc.all_engine_barrier(sems_to_clear=loop_sems)
        with nc.Fori(1, batch) as i:
            with nc.Block() as block:
                iteration(i, i - 1, (i + 1) % batch, block)
            nc.all_engine_barrier(sems_to_clear=loop_sems)
        with nc.Block() as block:
            iteration(None, batch - 1, None, block)


def kernel(**inputs):
    import concourse.bacc as bacc
    from concourse.bass_utils import run_bass_kernel_spmd

    g = {k: np.asarray(v) for k, v in inputs.items()}
    w = g["L0_attn_a_qkv_w"].transpose(1, 2, 0)

    def pairs(m):
        return m.reshape(PAIRS, P, -1).transpose(1, 0, 2)

    def columns(v):
        return v.reshape(-1, P).T

    def rows(v, times=1):
        return np.tile(v.reshape(1, -1), (P, times))

    eye = np.eye(P, dtype=np.float32)
    causal = np.zeros((P, TOK), np.float32)
    causal[:, TOK - P:] = np.triu(np.full((P, P), MASKED, np.float32), 1)
    eye_row = np.zeros((P, TOK), np.float32)
    eye_row[:, :P] = eye
    arrays = {
        "x": g["L0_attn_a_x"],
        "wq_t": pairs(w[:, 0:HD]), "wk_t": pairs(w[:, HD:2 * HD]),
        "wv": g["L0_attn_a_qkv_w"][:, :, 2 * HD:].reshape(P, HEADS * HD),
        "wo": pairs(g["L0_attn_a_out_w"]),
        "bq": columns(g["L0_attn_a_qkv_b"][:, 0:HD]), "bv": columns(g["L0_attn_a_qkv_b"][:, 2 * HD:]),
        "out_b": rows(g["L0_attn_a_out_b"]),
        "ffn_wt": g["L0_ffn_W"].T, "ffn_b": rows(g["L0_ffn_b"]), "up_t": g["L0_ffn_up_aux"].T,
        "lora_up_t": g["L0_ffn_lora_up"].T, "lora_down_t": g["L0_ffn_lora_down"].T,
        "down_aux": g["L0_ffn_down_aux"],
        "norm1": g["L0_attn_b_norm1_w"].reshape(P, 1), "norm2": g["L0_attn_b_norm2_w"].reshape(P, 1),
        "win_t": g["L0_attn_b_in_proj_w"].T,
        "conv_w": g["L0_attn_b_conv_w"].reshape(4, P, CONV).transpose(1, 0, 2),
        "conv_b": columns(g["L0_attn_b_conv_b"]),
        "dt_bias": rows(g["L0_attn_b_dt_bias"], NT), "a_log": rows(g["L0_attn_b_A_log"], NT),
        "d_col": columns(np.repeat(g["L0_attn_b_D"], HD)), "mnorm": columns(g["L0_attn_b_mnorm_w"]),
        "wmo": g["L0_attn_b_out_proj_w"].T.reshape(2, P, P).transpose(1, 0, 2),
        "w1": g["L0_attn_b_mlp_w1"].T, "b1": columns(g["L0_attn_b_mlp_b1"]),
        "w2": g["L0_attn_b_mlp_w2"].T.reshape(4, P, P).transpose(1, 0, 2), "b2": rows(g["L0_attn_b_mlp_b2"]),
        "mask": causal, "eye_row": eye_row,
    }
    nc = bacc.Bacc("TRN2", target_bir_lowering=False, num_devices=1)
    aps, ins = {}, {}
    for name, arr in arrays.items():
        arr = np.ascontiguousarray(arr)
        ins[f"in_{name}"] = arr
        aps[name] = nc.dram_tensor(f"in_{name}", arr.shape, mybir.dt.from_np(arr.dtype), kind="ExternalInput").ap()
    out = nc.dram_tensor("out", arrays["x"].shape, F32, kind="ExternalOutput").ap()
    layer(nc, aps, out)
    r = run_bass_kernel_spmd(nc, [ins], core_ids=[0])
    return r.results[0]["out"]
```

```python
from contextlib import ExitStack

import numpy as np

import concourse.bass as bass
from concourse import mybir

F32 = mybir.dt.float32
F32R = mybir.dt.float32r
ALU = mybir.AluOpType
ACT = mybir.ActivationFunctionType

P = 128
TOK = 512
NT = TOK // P
HEADS = 16
HD = 64
PAIRS = HEADS // 2
TRI = NT * (NT + 1) // 2 * P
MHEADS = 4
INNER = 256
CONV = 4
LN_EPS = 1e-5
BN_EPS = 1e-6
SCALE = HD ** -0.5
MASKED = -0.7 * float(np.finfo(np.float32).max)
LOG_TERMS = 8

TRI_AT = [P * t * (t + 1) // 2 for t in range(NT)]
BC_TILES = ((0,), (1, 3), (2,))
COL_AT = [P * (NT * j - j * (j - 1) // 2) for j in range(NT)]

NAMES = """
x_loaded x_mv x_rstd xn_ready hTh_ready hTl_ready front_gh front_gl
xb_ready v_full v_evac
g_full g_evac gh_ready gl_ready s_full sm_ready p_ready t_full pt_act pt_dve
rden_ready spread_ready r_full r_copied pv_done o_ready y_full x1_ready
misc_full0 misc_full1 misc_free0 misc_free1
dve_chain pool_chain
a_mv a_rstd n1_ready x1b_ready
b_mv b_r12 n_ready
dt_abs dt_exp dt_ready dta_ready da_ready
conv_ready tanh_ready ztanh_ready silu_ready m_ready
yz_ready y2_ready rs_ready ss2_ready r3_ready h3_ready x2b_ready
d_mv d_rstd n4_ready x3b_ready
out_dma
""".split()


def tile_cols(t):
    return P * (t + 1)


USES = NT - 1


def use_of(h, t):
    return USES * h + max(t - 1, 0)


def tiles_of(u):
    h, r = divmod(u, USES)
    return h, ((0, 1) if r == 0 else (r + 1,))


def bank_at(t):
    return P if t == 1 else 0


def layer(nc, a, out):
    with ExitStack() as ctx:
        def sb(name, shape, dt=F32):
            return ctx.enter_context(nc.sbuf_tensor(name, shape, dt))

        def bank(name):
            return ctx.enter_context(nc.psum_tensor(name, [P, 512], F32))

        psS = [bank("psS0"), bank("psS1")]
        psT = [bank("psT0"), bank("psT1")]
        psG = bank("psG")
        psO = bank("psO")
        psX = [bank("psX0"), bank("psX1")]

        mask = sb("mask", [P, TOK])
        eye_row = sb("eye_row", [P, TOK])
        ident = eye_row[:, 0:P]
        ones = sb("ones", [P, 1])
        neg_half = sb("neg_half", [P, NT])
        neg_one = sb("neg_one", [P, NT * MHEADS])
        PT = [sb(f"PT{i}", [P, NT, TOK]) for i in range(4)]
        wq_t = PT[0][:, 0:2, :].rearrange("p a (b e) -> p (a b) e", e=P)
        wk_t = PT[0][:, 2:4, :].rearrange("p a (b e) -> p (a b) e", e=P)
        wv = PT[1][:, 0:2, :].rearrange("p a c -> p (a c)")
        wo = sb("wo", [P, PAIRS, P])
        bq = sb("bq", [P, PAIRS, 2])
        bv = sb("bv", [P, PAIRS])
        row_out_b = sb("row_out_b", [P, P])
        ffn_wt = sb("ffn_wt", [P, P])
        ffn_b = sb("ffn_b", [P, P])
        up_t = sb("up_t", [50, P])
        lora_up_t = sb("lora_up_t", [4, 50])
        lora_down_t = sb("lora_down_t", [100, 4])
        down_aux = sb("down_aux", [100, P])
        norm1 = sb("norm1", [P, 1])
        norm2 = sb("norm2", [P, 1])
        win_t = sb("win_t", [P, 772])
        conv_w = sb("conv_w", [P, 4, CONV])
        conv_b = sb("conv_b", [P, 4])
        dt_bias = sb("dt_bias", [P, NT * MHEADS])
        a_log = sb("a_log", [P, NT * MHEADS])
        d_col = sb("d_col", [P, 2])
        mnorm = sb("mnorm", [P, 2])
        wmo = sb("wmo", [P, 2, P])
        w1 = sb("w1", [P, 4 * P])
        b1 = sb("b1", [P, 4])
        w2 = sb("w2", [P, 4, P])
        b2 = sb("b2", [P, P])
        exp_a = sb("exp_a", [P, NT * MHEADS])
        lora1 = sb("lora1", [4, P])
        lora2 = sb("lora2", [50, P])
        cq = sb("cq", [P, HEADS])
        mh = sb("mh", [P, HEADS, P], F32R)
        ml = sb("ml", [P, HEADS, P], F32R)
        wvh = sb("wvh", [P, HEADS * HD], F32R)
        wvl = sb("wvl", [P, HEADS * HD], F32R)

        xin = sb("xin", [P, NT, P])
        x_st = sb("x_st", [P, NT, 6])
        x_mv = sb("x_mv", [P, NT, 2])
        x_veps = sb("x_veps", [P, NT])
        x_rstd = sb("x_rstd", [P, NT])
        xn = sb("xn", [P, NT, P])
        hT = xn[:].rearrange("p t e -> p (t e)")
        xb = sb("xb", [P, NT, P])
        hTh = sb("hTh", [P, TOK], F32R)
        hTl = sb("hTl", [P, TOK], F32R)
        V = sb("V", [P, NT, HEADS * HD])
        G = sb("G", [P, TOK])
        Gh = [sb(f"Gh{i}", [P, TOK], F32R) for i in range(2)]
        Gl = [sb(f"Gl{i}", [P, TOK], F32R) for i in range(2)]
        Sm = [sb(f"Sm{i}", [P, TOK]) for i in range(3)]
        nb = sb("nb", [P, HEADS * NT])
        den = sb("den", [P, HEADS, NT])
        rden = sb("rden", [P, HEADS, NT])
        Pr = [sb(f"Pr{i}", [P, TRI]) for i in range(2)]
        R = sb("R", [P, TOK])
        x1 = sb("x1", [P, NT, P])

        st = sb("st", [P, NT, 6])
        a_mv = sb("a_mv", [P, NT, 2])
        a_veps = sb("a_veps", [P, NT])
        a_rstd = sb("a_rstd", [P, NT])
        n1 = sb("n1", [P, NT, P])
        x1b = sb("x1b", [P, NT, P])
        n1T = sb("n1T", [P, TOK])
        x2 = sb("x2", [P, NT, P])
        st2 = sb("st2", [P, NT, 6])
        b_mv = sb("b_mv", [P, NT, 2])
        b_veps = sb("b_veps", [P, NT])
        b_r1 = sb("b_r1", [P, NT])
        b_sq = sb("b_sq", [P, NT])
        b_r2 = sb("b_r2", [P, NT])
        b_r12 = sb("b_r12", [P, NT])
        u = sb("u", [P, NT, P])
        nn = sb("nn", [P, NT, P])
        nT = sb("nT", [P, TOK])
        dtx = sb("dtx", [P, NT * MHEADS])
        dt_abs = sb("dt_absx", [P, NT * MHEADS])
        dt_exp = sb("dt_expx", [P, NT * MHEADS])
        dt_s = sb("dt_s", [P, NT * MHEADS])
        dt_s2 = sb("dt_s2", [P, NT * MHEADS])
        dt_poly = sb("dt_poly", [P, NT * MHEADS])
        dta = sb("dta", [P, NT * MHEADS])
        dt = sb("dt", [P, NT * MHEADS])
        dA = sb("dA", [P, NT * MHEADS])
        pad = sb("pad", [P, 4, CONV - 1 + TOK])
        xbc = sb("xbc", [P, 4, TOK])
        zs = sb("zs", [P, 2, TOK])
        xdt = sb("xdt", [P, NT, INNER])
        bc = sb("bc", [P, TRI])
        Lall = sb("Lall", [P, 2 * TRI])
        L = [Lall[:, i * TRI:(i + 1) * TRI] for i in range(2)]

        def in_l(i):
            return Lall[:, i * TOK:(i + 1) * TOK].rearrange("p (t e) -> p t e", e=P)

        Mall = sb("Mall", [P, 2 * TRI])
        M = [Mall[:, i * TRI:(i + 1) * TRI] for i in range(2)]
        acc = [Mall[:, c * TOK:(c + 1) * TOK] for c in range(4)]
        gl = Mall[:, 0:4 * TOK].rearrange("p (f n) -> p f n", f=4)
        yd = sb("yd", [P, 2, TOK])
        yz = sb("yz", [P, 2, TOK])
        y2 = yd
        ss = sb("ss", [P, NT])
        rs = sb("rs", [P, NT])
        u2 = in_l(0)
        usq = in_l(1)
        ss2 = sb("ss2", [P, NT])
        r3_eps = sb("r3_eps", [P, NT])
        r3 = sb("r3", [P, NT])
        h3 = in_l(2)
        x2b = in_l(3)
        h3T = Lall[:, 4 * TOK:5 * TOK]
        x3 = x1b
        st4 = sb("st4", [P, NT, 6])
        d_mv = sb("d_mv", [P, NT, 2])
        d_veps = sb("d_veps", [P, NT])
        d_rstd = sb("d_rstd", [P, NT])
        n4 = n1
        x3b = nn
        n4T = n1T
        x4 = x2

        s = {n: ctx.enter_context(nc.semaphore(n)) for n in NAMES}
        nums = sorted(q.num for q in s.values())
        assert nums == list(range(nums[0], nums[0] + len(nums)))
        loop_sems = range(nums[0], nums[-1] + 1)
        misc_full = [s["misc_full0"], s["misc_full1"]]
        misc_free = [s["misc_free0"], s["misc_free1"]]

        qk_loaded = ctx.enter_context(nc.semaphore("qk_weights_loaded"))
        eye_loaded = ctx.enter_context(nc.semaphore("identity_loaded"))
        v_loaded = ctx.enter_context(nc.semaphore("v_weights_loaded"))
        loaded = ctx.enter_context(nc.semaphore("attention_weights_loaded"))
        tail_loaded = ctx.enter_context(nc.semaphore("tail_weights_loaded"))
        su_pe = ctx.enter_context(nc.semaphore("setup_products"))
        su_dve = ctx.enter_context(nc.semaphore("setup_dve"))
        su_act = ctx.enter_context(nc.semaphore("setup_act"))
        su_pool = ctx.enter_context(nc.semaphore("setup_pool"))

        attention_loads = [(mask, "mask"), (wo, "wo"), (bv, "bv"), (row_out_b, "out_b")]
        tail_loads = [(ffn_wt, "ffn_wt"), (ffn_b, "ffn_b"), (up_t, "up_t"), (lora_up_t, "lora_up_t"),
                      (lora_down_t, "lora_down_t"), (down_aux, "down_aux"), (norm1, "norm1"), (norm2, "norm2"),
                      (win_t, "win_t"), (w1, "w1"), (w2, "w2"), (wmo, "wmo"), (conv_w, "conv_w"), (conv_b, "conv_b"),
                      (dt_bias, "dt_bias"), (a_log, "a_log"), (d_col, "d_col"), (mnorm, "mnorm"), (b1, "b1"), (b2, "b2")]
        QK_LOADED = 3 * 16
        ATTENTION_LOADED = 16 * len(attention_loads)
        TAIL_LOADED = 16 * len(tail_loads)
        SU_M = (1, 3, 4, 5)
        SU_MH = (1, 3, 4, 5)
        four = [(slice(8 * k + odd, 8 * k + odd + 7, 2), (psT if odd else psS)[k]) for k in range(2) for odd in range(2)]

        STEPS = HEADS + 3
        SLOTS = STEPS * NT
        FOLD_AT = {8: ["lora1"], 10: ["lora2"], 12: ["lora3"]}
        PE_AT = {
            4: ["n1T"], 6: ["ffn1"], 11: ["nT"], 12: ["dt"], 17: ["xc0"], 18: ["xc1", "xc2"], 19: ["z0"],
            20: ["xc3"], 22: ["z1"], 24: ["xdt0"], 26: ["xdt1"], 30: ["bc0"], 31: ["bc1"],
            35: ["bc2", "da0"], 36: ["da1"], 39: ["da2"], 43: ["y0.0", "y0.1"], 45: ["da3"],
            51: ["y1.0", "y1.1"], 53: ["mo.0"], 54: ["ss"], 55: ["mo.1"], 63: ["h3T"], 65: ["g0", "g1"],
            66: ["g2", "nxT"], 67: ["g3"], 69: ["mlp.0", "gx", "mlp.1"], 70: ["n4T", "ffn2"]}
        FRONT_USES = ("nxT", "gx")
        AT = dict(
            stats1=0, rstd1=2, norm1=4, n1T=5, x2=6, r12=8, u=17, n=10, nT=11, dtx=12,
            pads=(17, 18, 19, 20), softplus=11, dt_exp=13, softplus_end=17,
            conv=(18, 18, 19, 19, 19, 20, 21, 21, 21, 23, 24, 25), tanh=(19, 20, 23, 24),
            silu=(20, 22, 25, 27), ztanh=(19, 21), zsilu=(20, 24), decay=22, xdt=(28, 29), bc=(30, 31, 33),
            scan=(34, 35, 37, 38, 41, 43, 46, 47), mul=(35, 37, 38, 39, 43, 44, 48, 49), y=(46, 51),
            ysq=(47, 50), ss=54, rs=56, u2=56, ssum=59, r3=61, h3=62, x2b=67, h3T=63, gelu=(63, 68), x3=68,
            rstd4=67, norm4=72, x3b=67, n4T=74, x4=72, front_stats=39, front_rstd=39, front_norm=45,
            front_h=68, front_split=67, front_g=69, front_gh=75, front_gl=71)
        CONV_ORDER = [(0, 0), (0, 1), (1, 0), (0, 2), (1, 1), (2, 0), (1, 2), (2, 1), (2, 2), (3, 0), (3, 1), (3, 2)]
        G_AT = dict(project=0, copy=0, split=2, rest=2)
        V_AT = 0
        V_LATER = 0
        PAIR_AT = dict(invert=6, spread=6, turn_r=11, copy_r=11, attend=(10, 11, 12, 13), normalise=14)
        LAST_AT = dict(invert=7, spread=5, turn_r=9, copy_r=9, attend=(8, 8, 8, 9), normalise=9)
        PROJECT = 70
        ACT_TILES = 3

        def pair_slot(p, stage):
            return NT * (2 * p + 1) + (PAIR_AT if p < PAIRS - 1 else LAST_AT)[stage]

        def pairs_at(k, stage):
            return [p for p in range(PAIRS) if pair_slot(p, stage) == k]

        def attend_at(k):
            return [(p, j) for p in range(PAIRS) for j in range(NT)
                    if NT * (2 * p + 1) + (PAIR_AT if p < PAIRS - 1 else LAST_AT)["attend"][j] == k]

        def iteration(ia, it, nxt, block):
            att, tail, front = ia is not None, it is not None, nxt is not None
            fold = att and not tail
            setup = front and not att
            uses = []
            for k in range(SLOTS):
                if att and PAIRS - 1 in pairs_at(k, "turn_r"):
                    uses.append("r")
                if fold:
                    uses += FOLD_AT.get(k, [])
                uses += [n.split(".")[0] for n in PE_AT.get(k, [])
                         if (front if n in FRONT_USES else tail) and n[-2:] not in (".1", ".2", ".3")]
            order = {name: n for n, name in enumerate(uses)}

            def X(name):
                return psX[order[name] % 2]

            def fill(pe, name):
                n = order[name]
                if n >= 2:
                    pe.wait_ge(misc_free[n % 2], n // 2)
                return psX[n % 2]

            def full(name):
                return misc_full[order[name] % 2]

            def free(name):
                return misc_free[order[name] % 2]

            def count(name):
                return order[name] // 2 + 1

            def wait_full(eng, name):
                eng.wait_ge(full(name), count(name))
                return X(name)

            def wait_read(eng, name):
                eng.wait_ge(free(name), count(name))

            def wait_pt(eng, h, t):
                if t < ACT_TILES:
                    eng.wait_ge(s["pt_act"], ACT_TILES * h + t + 1)
                else:
                    eng.wait_ge(s["pt_dve"], (NT - ACT_TILES) * h + t - ACT_TILES + 1)

            @block.sync
            def _(sp):
                if setup:
                    sp.dma_start(wq_t, a["wq_t"]).then_inc(qk_loaded, 16)
                    sp.dma_start(bq[:], a["bq"]).then_inc(qk_loaded, 16)
                    sp.dma_start(wv, a["wv"]).then_inc(v_loaded, 16)
                    for t, name in attention_loads:
                        sp.dma_start(t[:], a[name]).then_inc(loaded, 16)
                    for t, name in tail_loads:
                        sp.dma_start(t[:], a[name]).then_inc(tail_loaded, 16)
                if att and front:
                    sp.wait_ge(s["xb_ready"], NT)
                    sp.dma_start(xin[:], a["x"][nxt].rearrange("(t p) e -> p t e", p=P)).then_inc(s["x_loaded"], 16)
                if tail:
                    wait_read(sp, "ffn2")
                    sp.dma_start(out[it].rearrange("(t p) e -> p t e", p=P), x4[:]).then_inc(s["out_dma"], 16)
                    sp.wait_ge(s["out_dma"], 16)

            def three_passes(ps, lhs, rhs):
                (lh, ll), (rh, rl) = lhs, rhs
                nc.tensor.matmul(ps, lh, rh, start=True, stop=False)
                nc.tensor.matmul(ps, lh, rl, start=False, stop=False)
                return nc.tensor.matmul(ps, ll, rh, start=False, stop=True)

            @block.tensor
            def _(pe):
                def products_m(n):
                    heads, ps = four[n]
                    for h in range(heads.start, heads.stop, 2):
                        half = slice(HD * (h % 2), HD * (h % 2) + HD)
                        at = P * (h % 8 // 2)
                        last = nc.tensor.matmul(ps[:, at:at + P], wq_t[half, h // 2, :], wk_t[half, h // 2, :],
                                                start=True, stop=True)
                    last.then_inc(su_pe, 1)

                def products_bias():
                    for p in range(PAIRS):
                        last = nc.tensor.matmul(psG[:, 2 * p:2 * p + 2], wk_t[:, p, :], bq[:, p, :],
                                                start=True, stop=True)
                    last.then_inc(su_pe, 1)

                def products_out_bias():
                    pe.wait_ge(loaded, ATTENTION_LOADED)
                    for p in range(PAIRS):
                        last = nc.tensor.matmul(psO[:, 0:P], bv[:, p:p + 1].to_broadcast([P, P]), wo[:, p, :],
                                                start=(p == 0), stop=(p == PAIRS - 1))
                    last.then_inc(su_pe, 1)

                in_g = dict(g=0, r=0)

                def project_g(h):
                    if in_g["g"]:
                        pe.wait_ge(s["g_evac"], in_g["g"])
                    if in_g["r"]:
                        pe.wait_ge(s["r_copied"], in_g["r"])
                    in_g["g"] += 1
                    three_passes(psG[:], (mh[:, h, :], ml[:, h, :]), (hTh[:], hTl[:])).then_inc(s["g_full"], 1)

                def project_v(n):
                    t, half = divmod(n, 2)
                    if n >= 1:
                        pe.wait_ge(s["v_evac"], n)
                    cols = slice(512 * half, 512 * half + 512)
                    three_passes(psO[:], (hTh[:, P * t:P * t + P], hTl[:, P * t:P * t + P]),
                                 (wvh[:, cols], wvl[:, cols])).then_inc(s["v_full"], 1)

                def scores(u):
                    h, tiles = tiles_of(u)
                    if u >= 2:
                        before, read = tiles_of(u - 2)
                        pe.wait_ge(s["sm_ready"], NT * before + read[-1] + 1)
                    if tiles[0] == 0 and h >= 1:
                        pe.wait_ge(s["gh_ready"], h)
                        pe.wait_ge(s["gl_ready"], h)
                    for t in tiles:
                        w = tile_cols(t)
                        q = slice(P * t, P * t + P)
                        last = three_passes(psS[u % 2][:, bank_at(t):bank_at(t) + w], (Gh[h % 2][:, q], Gl[h % 2][:, q]),
                                            (hTh[:, 0:w], hTl[:, 0:w]))
                    last.then_inc(s["s_full"], 1)

                def turn(u):
                    h, tiles = tiles_of(u)
                    if u >= 2:
                        before, copied = tiles_of(u - 2)
                        for t in copied:
                            wait_pt(pe, before, t)
                    pe.wait_ge(s["p_ready"], NT * h + tiles[-1] + 1)
                    for t in tiles:
                        for j in range(t + 1):
                            last = nc.tensor.transpose(psT[u % 2][:, bank_at(t) + P * j:bank_at(t) + P * j + P],
                                                       Pr[h % 2][:, TRI_AT[t] + P * j:TRI_AT[t] + P * j + P], ident)
                    last.then_inc(s["t_full"], 1)

                def turn_r(p):
                    if p < PAIRS - 1:
                        ps = psG
                        pe.wait_ge(s["g_evac"], in_g["g"])
                        if in_g["r"]:
                            pe.wait_ge(s["r_copied"], in_g["r"])
                        in_g["r"] += 1
                    else:
                        ps = fill(pe, "r")
                    pe.wait_ge(s["spread_ready"], p + 1)
                    for t in range(NT):
                        last = nc.tensor.transpose(ps[:, P * t:P * t + P], R[:, P * t:P * t + P], ident)
                    last.then_inc(s["r_full"] if p < PAIRS - 1 else full("r"), 1)

                def attend(p, j):
                    if j == 0:
                        wait_pt(pe, 2 * p + 1, ACT_TILES - 1)
                        wait_pt(pe, 2 * p + 1, NT - 1)
                        if p >= 1:
                            pe.wait_ge(s["o_ready"], p)
                        else:
                            pe.wait_ge(s["v_evac"], 2 * NT)
                    for hh in range(2):
                        h = 2 * p + hh
                        last = nc.tensor.matmul(psO[HD * hh:HD * hh + HD, P * j:TOK], V[:, j, HD * h:HD * h + HD],
                                                PT[h % 4][:, j, P * j:TOK], start=(j == 0), stop=(j == NT - 1),
                                                skip_group_check=True)
                    if j == NT - 1:
                        last.then_inc(s["pv_done"], 1)

                def project_out(first, last_pair):
                    pe.wait_ge(s["o_ready"], last_pair)
                    if first == 0:
                        pe.wait_ge(s["g_evac"], HEADS - 1)
                        pe.wait_ge(s["r_copied"], PAIRS - 1)
                    for t in range(NT):
                        for p in range(first, last_pair):
                            last = nc.tensor.matmul(psG[:, P * t:P * t + P], V[:, t, P * p:P * p + P], wo[:, p, :],
                                                    start=(p == 0 and t == 0), stop=(p == PAIRS - 1),
                                                    skip_group_check=True)
                    last.then_inc(s["y_full"], 1)

                def transposed(name, src):
                    ps = fill(pe, name)
                    for t in range(NT):
                        last = nc.tensor.transpose(ps[:, P * t:P * t + P], src[:, t, :], ident)
                    last.then_inc(full(name), 1)

                def linear(name, lhsT, w):
                    ps = fill(pe, name)
                    for t in range(NT):
                        last = nc.tensor.matmul(ps[:, P * t:P * t + P], lhsT[:, P * t:P * t + P], w, start=True, stop=True)
                    last.then_inc(full(name), 1)

                def channels(name, w, x):
                    ps = fill(pe, name)
                    nc.tensor.matmul(ps[:], w, x, start=True, stop=True).then_inc(full(name), 1)

                def tail_use(name, part):
                    if name == "n1T":
                        pe.wait_ge(s["n1_ready"], NT)
                        transposed(name, n1)
                    elif name == "ffn1":
                        wait_read(pe, "n1T")
                        linear(name, n1T, ffn_wt[:])
                    elif name == "nT":
                        pe.wait_ge(s["n_ready"], NT)
                        transposed(name, nn)
                    elif name == "dt":
                        wait_read(pe, "nT")
                        ps = fill(pe, name)
                        for t in range(NT):
                            last = nc.tensor.matmul(ps[:, MHEADS * t:MHEADS * t + MHEADS], nT[:, P * t:P * t + P],
                                                    win_t[:, 768:772], start=True, stop=True)
                        last.then_inc(full(name), 1)
                    elif name[:2] == "xc":
                        c = int(name[2])
                        channels(name, win_t[:, INNER + P * c:INNER + P * c + P], nT[:])
                    elif name[0] == "z":
                        c = int(name[1])
                        channels(name, win_t[:, P * c:P * c + P], nT[:])
                    elif name[:3] == "xdt":
                        k = int(name[3])
                        pe.wait_ge(s["silu_ready"], 2)
                        ps = fill(pe, name)
                        for tt in range(2):
                            for c in range(2):
                                t = 2 * k + tt
                                last = nc.tensor.transpose(ps[:, INNER * tt + P * c:INNER * tt + P * c + P],
                                                           xbc[:, c, P * t:P * t + P], ident)
                        last.then_inc(full(name), 1)
                    elif name[:2] == "bc":
                        pe.wait_ge(s["silu_ready"], 4)
                        ps = fill(pe, name)
                        at = 0
                        for j in BC_TILES[int(name[2])]:
                            w = TOK - P * j
                            last = nc.tensor.matmul(ps[:, at:at + w], xbc[:, 2, P * j:P * j + P], xbc[:, 3, P * j:TOK],
                                                    start=True, stop=True)
                            at += w
                        last.then_inc(full(name), 1)
                    elif name[:2] == "da":
                        pe.wait_ge(s["da_ready"], 1)
                        ps = fill(pe, name)
                        for t in range(NT):
                            k = MHEADS * t + int(name[2])
                            last = nc.tensor.transpose(ps[:, P * t:P * t + P], dA[:, k:k + 1].to_broadcast([P, P]), ident)
                        last.then_inc(full(name), 1)
                    elif name in ("y0", "y1"):
                        p = int(name[1])
                        if part == 0:
                            fill(pe, name)
                            for k in range(2):
                                wait_read(pe, f"xdt{k}")
                            pe.wait_ge(s["m_ready"], 4 * p + 4)
                        ps = X(name)
                        for j in (0,) if part == 0 else (1, 2, 3):
                            for hh in range(2):
                                h = 2 * p + hh
                                last = nc.tensor.matmul(ps[HD * hh:HD * hh + HD, P * j:TOK], xdt[:, j, HD * h:HD * h + HD],
                                                        M[h % 2][:, COL_AT[j]:COL_AT[j] + TOK - P * j], start=(j == 0),
                                                        stop=(j == NT - 1), skip_group_check=True)
                        if part == 1:
                            last.then_inc(full(name), 1)
                    elif name == "ss":
                        ps = fill(pe, name)
                        pe.wait_ge(s["y2_ready"], 2)
                        for t in range(NT):
                            for c in range(2):
                                last = nc.tensor.matmul(ps[:, t:t + 1], y2[:, c, P * t:P * t + P], ones[:],
                                                        start=(c == 0), stop=(c == 1), skip_group_check=True)
                        last.then_inc(full(name), 1)
                    elif name == "mo":
                        ps = X(name)
                        if part == 0:
                            fill(pe, name)
                            pe.wait_ge(s["yz_ready"], 2)
                        for t in (2 * part, 2 * part + 1):
                            for c in range(2):
                                last = nc.tensor.matmul(ps[:, P * t:P * t + P], yz[:, c, P * t:P * t + P], wmo[:, c, :],
                                                        start=(c == 0), stop=(c == 1), skip_group_check=True)
                        if part == 1:
                            last.then_inc(full(name), 1)
                    elif name == "h3T":
                        pe.wait_ge(s["h3_ready"], NT)
                        transposed(name, h3)
                    elif name in ("g0", "g1", "g2", "g3"):
                        f = int(name[1])
                        wait_read(pe, "h3T")
                        channels(name, w1[:, P * f:P * f + P], h3T)
                    elif name == "mlp":
                        ps = X(name)
                        if part == 0:
                            fill(pe, name)
                            for f in range(4):
                                wait_read(pe, f"g{f}")
                        for t in (2 * part, 2 * part + 1):
                            for f in range(4):
                                last = nc.tensor.matmul(ps[:, P * t:P * t + P], gl[:, f, P * t:P * t + P], w2[:, f, :],
                                                        start=(f == 0), stop=(f == 3), skip_group_check=True)
                        if part == 1:
                            last.then_inc(full(name), 1)
                    elif name == "n4T":
                        pe.wait_ge(s["n4_ready"], NT)
                        transposed(name, n4)
                    elif name == "ffn2":
                        wait_read(pe, "n4T")
                        linear(name, n4T, ffn_wt[:])

                def front_use(name):
                    if name == "nxT":
                        pe.wait_ge(s["xn_ready"], NT)
                        transposed(name, xn)
                    elif name == "gx":
                        if setup:
                            pe.wait_ge(su_act, 1)
                            pe.wait_ge(su_dve, 1)
                        pe.wait_ge(s["hTh_ready"], 1)
                        pe.wait_ge(s["hTl_ready"], 1)
                        ps = fill(pe, name)
                        three_passes(ps[:], (mh[:, 0, :], ml[:, 0, :]), (hTh[:], hTl[:])).then_inc(full(name), 1)

                def fold_use(name):
                    ps = fill(pe, name)
                    if name == "lora1":
                        pe.wait_ge(tail_loaded, TAIL_LOADED)
                        last = nc.tensor.matmul(ps[0:4, 0:P], lora_down_t[:], down_aux[:], start=True, stop=True)
                    elif name == "lora2":
                        wait_read(pe, "lora1")
                        last = nc.tensor.matmul(ps[0:50, 0:P], lora_up_t[:], lora1[:], start=True, stop=True)
                    else:
                        wait_read(pe, "lora2")
                        last = nc.tensor.matmul(ps[:, 0:P], lora2[:], up_t[:], start=True, stop=True)
                    last.then_inc(full(name), 1)

                for k in range(SLOTS):
                    step, t = divmod(k, NT)
                    if fold:
                        for name in FOLD_AT.get(k, []):
                            fold_use(name)
                    if att:
                        if step < HEADS and t != 1:
                            scores(use_of(step, t))
                        if 1 <= step <= HEADS and t != 1:
                            turn(use_of(step - 1, t))
                        if 0 <= k - V_AT < 2 * NT:
                            project_v(k - V_AT)
                        for p in pairs_at(k, "turn_r"):
                            turn_r(p)
                        if t == G_AT["project"] and step + 1 < HEADS:
                            project_g(step + 1)
                        for p, j in attend_at(k):
                            attend(p, j)
                        if k == PROJECT:
                            project_out(0, PAIRS - 1)
                    for name in PE_AT.get(k, []):
                        if name in FRONT_USES:
                            if setup and name == "nxT":
                                pe.wait_ge(qk_loaded, QK_LOADED)
                                products_m(0)
                                pe.wait_ge(eye_loaded, 16)
                            if front:
                                front_use(name)
                            if setup and name == "nxT":
                                products_bias()
                            if setup and name == "gx":
                                for n in (1, 2, 3):
                                    products_m(n)
                        elif tail:
                            base, _, part = name.partition(".")
                            tail_use(base, int(part or 0))
                if setup:
                    products_out_bias()
                if att:
                    project_out(PAIRS - 1, PAIRS)

            @block.scalar
            def _(act):
                def copy_m(n):
                    act.wait_ge(su_pe, SU_M[n])
                    heads, ps = four[n]
                    nc.scalar.copy(mh[:, heads, :], ps[:].rearrange("p (h e) -> p h e", e=P)).then_inc(su_act, 1)

                if setup:
                    act.dma_start(xin[:], a["x"][0].rearrange("(t p) e -> p t e", p=P)).then_inc(s["x_loaded"], 16)
                    act.dma_start(wk_t, a["wk_t"]).then_inc(qk_loaded, 16)
                    act.dma_start(eye_row[:], a["eye_row"]).then_inc(eye_loaded, 16)
                    copy_m(0)
                def copy_g(h):
                    act.wait_ge(s["g_full"], h)
                    if h >= 2:
                        act.wait_ge(s["gh_ready"], h - 1)
                        act.wait_ge(s["gl_ready"], h - 1)
                    nc.scalar.activation(G[:], psG[:], ACT.Identity, bias=cq[:, h:h + 1]).then_inc(s["g_evac"], 1)

                def copy_v(n):
                    act.wait_ge(s["v_full"], n + 1)
                    nc.scalar.copy(V[:, n // 2, 0:512], psO[:]).then_inc(s["v_evac"], 1)

                def probs(h, t):
                    n = NT * h + t
                    act.wait_ge(s["sm_ready"], n + 1)
                    if h >= 2:
                        act.wait_ge(s["t_full"], use_of(h - 2, t) + 1)
                    w = tile_cols(t)
                    nc.scalar.activation(Pr[h % 2][:, TRI_AT[t]:TRI_AT[t] + w], Sm[n % 3][:, 0:w], ACT.Exp,
                                         bias=nb[:, n:n + 1], scale=-1.0,
                                         accum_out=den[:, h, t:t + 1]).then_inc(s["p_ready"], 1)

                def copy_t(h, t):
                    act.wait_ge(s["t_full"], use_of(h, t) + 1)
                    if h >= 4:
                        act.wait_ge(s["pv_done"], (h - 4) // 2 + 1)
                    src = psT[use_of(h, t) % 2][:, bank_at(t):bank_at(t) + tile_cols(t)].rearrange("p (j q) -> p j q", q=P)
                    nc.scalar.copy(PT[h % 4][:, 0:t + 1, P * t:P * t + P], src).then_inc(s["pt_act"], 1)

                def copy_r(p):
                    if p < PAIRS - 1:
                        act.wait_ge(s["r_full"], p + 1)
                        nc.scalar.copy(R[:], psG[:]).then_inc(s["r_copied"], 1)
                    else:
                        evacuate(R[:], "r")

                def evacuate(dst, name):
                    ps = wait_full(act, name)
                    nc.scalar.copy(dst, ps[:]).then_inc(free(name), 1)

                def tail_part(k):
                    if k == AT["n1T"]:
                        evacuate(n1T[:], "n1T")
                    if k == AT["nT"]:
                        evacuate(nT[:], "nT")
                    if k in AT["pads"]:
                        c = AT["pads"].index(k)
                        ps = wait_full(act, f"xc{c}")
                        nc.scalar.copy(pad[:, c, CONV - 1:], ps[:])
                        nc.scalar.activation(acc[c], ps[:], ACT.Identity, bias=conv_b[:, c:c + 1],
                                             scale=conv_w[:, c, CONV - 1:CONV]).then_inc(free(f"xc{c}"), 1)
                    if k == AT["dt_exp"]:
                        act.wait_ge(s["dt_abs"], 1)
                        nc.scalar.activation(dt_exp[:], dt_abs[:], ACT.Exp, scale=-1.0).then_inc(s["dt_exp"], 1)
                    if k in AT["tanh"]:
                        c = AT["tanh"].index(k)
                        act.wait_ge(s["conv_ready"], c + 1)
                        nc.scalar.activation(xbc[:, c, :], acc[c], ACT.Tanh).then_inc(s["tanh_ready"], 1)
                    if k in AT["ztanh"]:
                        c = AT["ztanh"].index(k)
                        ps = wait_full(act, f"z{c}")
                        nc.scalar.activation(zs[:, c, :], ps[:], ACT.Tanh).then_inc(s["ztanh_ready"], 1)
                    if k == AT["decay"]:
                        act.wait_ge(s["dta_ready"], 1)
                        nc.scalar.activation(dA[:], dta[:], ACT.Exp, scale=-1.0).then_inc(s["da_ready"], 1)
                    if k in AT["bc"]:
                        n = AT["bc"].index(k)
                        ps = wait_full(act, f"bc{n}")
                        at = 0
                        for j in BC_TILES[n]:
                            w = TOK - P * j
                            last = nc.scalar.copy(bc[:, COL_AT[j]:COL_AT[j] + w], ps[:, at:at + w])
                            at += w
                        last.then_inc(free(f"bc{n}"), 1)
                    if k in AT["ysq"]:
                        c = AT["ysq"].index(k)
                        act.wait_ge(s["yz_ready"], c + 1)
                        nc.scalar.activation(y2[:, c, :], yz[:, c, :], ACT.Square).then_inc(s["y2_ready"], 1)
                    if k == AT["ssum"]:
                        wait_read(act, "mo")
                        for t in range(NT):
                            nc.scalar.activation(usq[:, t, :], u2[:, t, :], ACT.Square,
                                                 accum_out=ss2[:, t:t + 1]).then_inc(s["ss2_ready"], 1)
                    if k == AT["h3T"]:
                        evacuate(h3T, "h3T")
                    if k in AT["gelu"]:
                        for f in (0, 1) if k == AT["gelu"][0] else (2, 3):
                            ps = wait_full(act, f"g{f}")
                            nc.scalar.activation(gl[:, f, :], ps[:], ACT.Gelu, bias=b1[:, f:f + 1]).then_inc(free(f"g{f}"), 1)
                    if k == AT["n4T"]:
                        evacuate(n4T[:], "n4T")

                def front_part(k):
                    if k == AT["front_h"]:
                        evacuate(hT, "nxT")
                        if setup:
                            act.wait_ge(su_pe, 2)
                            nc.scalar.copy(cq[:], psG[:, 0:HEADS]).then_inc(su_act, 1)
                    if k == AT["front_g"]:
                        ps = wait_full(act, "gx")
                        if setup:
                            act.wait_ge(su_act, 2)
                        if att:
                            act.wait_ge(s["gh_ready"], HEADS - 1)
                            act.wait_ge(s["gl_ready"], HEADS - 1)
                        nc.scalar.activation(G[:], ps[:], ACT.Identity, bias=cq[:, 0:1]).then_inc(free("gx"), 1)
                        if setup:
                            for n in (1, 2, 3):
                                copy_m(n)
                            act.wait_ge(v_loaded, 16)
                            nc.scalar.copy(wvh[:], wv).then_inc(su_act, 1)

                def fold_part(k):
                    if "lora1" in FOLD_AT.get(k, []):
                        ps = wait_full(act, "lora1")
                        nc.scalar.copy(lora1[:], ps[0:4, 0:P]).then_inc(free("lora1"), 1)
                        act.wait_ge(tail_loaded, TAIL_LOADED)
                        nc.scalar.activation(exp_a[:], a_log[:], ACT.Exp)
                    if "lora2" in FOLD_AT.get(k, []):
                        ps = wait_full(act, "lora2")
                        nc.scalar.copy(lora2[:], ps[0:50, 0:P]).then_inc(free("lora2"), 1)

                for k in range(SLOTS):
                    step, t = divmod(k, NT)
                    if fold:
                        fold_part(k)
                    if att:
                        if step < HEADS:
                            probs(step, t)
                        if 0 <= k - V_AT - V_LATER < 2 * NT and (k - V_AT - V_LATER) % 2 == 0:
                            copy_v(k - V_AT - V_LATER)
                        for p in pairs_at(k, "copy_r"):
                            copy_r(p)
                        if t < ACT_TILES and 1 <= step <= HEADS:
                            copy_t(step - 1, t)
                        if t == G_AT["copy"] and step + 1 < HEADS:
                            copy_g(step + 1)
                    if tail:
                        tail_part(k)
                    if front:
                        front_part(k)

            @block.vector
            def _(dve):
                def low_m(n):
                    dve.wait_ge(su_act, SU_MH[n])
                    heads, ps = four[n]
                    nc.vector.tensor_tensor(ml[:, heads, :], ps[:].rearrange("p (h e) -> p h e", e=P),
                                            mh[:, heads, :].bitcast(F32), ALU.subtract).then_inc(su_dve, 1)

                chained = [0]

                def chain(last):
                    chained[0] += 1
                    last.then_inc(s["dve_chain"], 1)
                    dve.wait_ge(s["dve_chain"], chained[0])

                def flat(x):
                    return x[:, :, :].rearrange("p t e -> p (t e)")

                def statistics(x, stats, mv, ready):
                    for t in range(NT):
                        last = nc.vector.bn_stats(stats[:, t, :], x[:, t, :])
                    chain(last)
                    for t in range(NT):
                        last = nc.vector.bn_aggr(mv[:, t, :], stats[:, t, :])
                    last.then_inc(ready, 1)

                def normalise(dst, x, mv, rstd, ready):
                    for t in range(NT):
                        nc.vector.tensor_scalar(dst[:, t, :], x[:, t, :], mv[:, t, 0:1], rstd[:, t:t + 1],
                                                ALU.subtract, ALU.mult).then_inc(ready, 1)

                def copy_v(n):
                    dve.wait_ge(s["v_full"], n + 1)
                    nc.vector.tensor_copy(V[:, n // 2, 512:1024], psO[:]).then_inc(s["v_evac"], 1)

                def split_g(h):
                    dve.wait_ge(s["g_evac"], h)
                    if h >= 2:
                        dve.wait_ge(s["s_full"], USES * (h - 1))
                    if h >= 3:
                        dve.wait_ge(s["gl_ready"], h - 2)
                    nc.vector.tensor_copy(Gh[h % 2][:], G[:]).then_inc(s["gh_ready"], 1)

                def mask_and_max(h, t):
                    n = NT * h + t
                    dve.wait_ge(s["s_full"], use_of(h, t) + 1)
                    if n >= 3:
                        dve.wait_ge(s["p_ready"], n - 2)
                    w = tile_cols(t)
                    nc.vector.tensor_tensor_reduce(
                        out=Sm[n % 3][:, 0:w], in0=psS[use_of(h, t) % 2][:, bank_at(t):bank_at(t) + w], in1=mask[:, TOK - w:TOK], scale=-SCALE,
                        scalar=3.0e38, op0=ALU.add, op1=ALU.min, accum_out=nb[:, n:n + 1]).then_inc(s["sm_ready"], 1)

                def copy_t(h, t):
                    dve.wait_ge(s["t_full"], use_of(h, t) + 1)
                    if h >= 4:
                        dve.wait_ge(s["pv_done"], (h - 4) // 2 + 1)
                    src = psT[use_of(h, t) % 2][:, bank_at(t):bank_at(t) + tile_cols(t)].rearrange("p (j q) -> p j q", q=P)
                    nc.vector.tensor_copy(PT[h % 4][:, 0:t + 1, P * t:P * t + P], src).then_inc(s["pt_dve"], 1)

                def invert(p):
                    dve.wait_ge(s["p_ready"], NT * (2 * p + 2))
                    nc.vector.reciprocal(rden[:, 2 * p:2 * p + 2, :], den[:, 2 * p:2 * p + 2, :]).then_inc(s["rden_ready"], 1)

                def normalise_o(p):
                    dve.wait_ge(s["pv_done"], p + 1)
                    if p < PAIRS - 1:
                        dve.wait_ge(s["r_copied"], p + 1)
                    else:
                        wait_read(dve, "r")
                    nc.vector.tensor_tensor(V[:, :, P * p:P * p + P], psO[:].rearrange("p (t q) -> p t q", q=P),
                                            R[:].rearrange("p (t q) -> p t q", q=P), ALU.mult).then_inc(s["o_ready"], 1)

                def end():
                    dve.wait_ge(s["y_full"], 2)
                    dve.wait_ge(s["xb_ready"], NT)
                    if tail:
                        dve.wait_ge(s["n1_ready"], NT)
                        dve.wait_ge(s["x1b_ready"], NT)
                    nc.vector.tensor_tensor(flat(x1), psG[:], flat(xb), ALU.add).then_inc(s["x1_ready"], 1)
                    dve.wait_ge(s["x1_ready"], 1)

                def add_to(dst, name, x, ready, n):
                    ps = wait_full(dve, name)
                    dve.wait_ge(ready, n)
                    nc.vector.tensor_tensor(flat(dst), ps[:], flat(x), ALU.add).then_inc(free(name), 1)
                    wait_read(dve, name)

                written = {}

                def convolve(c, tap):
                    if tap == 0:
                        wait_read(dve, f"xc{c}")
                    else:
                        dve.wait_ge(s["dve_chain"], written[c])
                    last = nc.vector.scalar_tensor_tensor(
                        out=acc[c], in0=pad[:, c, tap:tap + TOK], scalar=conv_w[:, c, tap:tap + 1], in1=acc[c],
                        op0=ALU.mult, op1=ALU.add)
                    if tap < CONV - 2:
                        chained[0] += 1
                        written[c] = chained[0]
                        last.then_inc(s["dve_chain"], 1)
                    else:
                        last.then_inc(s["conv_ready"], 1)

                def scan(h, js):
                    ps = wait_full(dve, f"da{h}")
                    if h >= 2:
                        dve.wait_ge(s["m_ready"], 2 * h - 2)
                    for j in js:
                        w = TOK - P * j
                        last = nc.vector.tensor_tensor_scan(L[h % 2][:, COL_AT[j]:COL_AT[j] + w], ps[:, P * j:TOK],
                                                            eye_row[:, 0:w], 0.0, ALU.mult, ALU.add)
                    if NT - 1 in js:
                        last.then_inc(free(f"da{h}"), 1)

                def tail_part(k):
                    if k == AT["stats1"]:
                        statistics(x1, st, a_mv, s["a_mv"])
                    if k == AT["norm1"]:
                        dve.wait_ge(s["a_mv"], 1)
                        dve.wait_ge(s["a_rstd"], 1)
                        normalise(n1, x1, a_mv, a_rstd, s["n1_ready"])
                    if k == AT["x2"]:
                        add_to(x2, "ffn1", x1b, s["x1b_ready"], NT)
                        statistics(x2, st2, b_mv, s["b_mv"])
                    if k == AT["u"]:
                        dve.wait_ge(s["b_mv"], 1)
                        dve.wait_ge(s["b_r12"], 1)
                        for t in range(NT):
                            nc.vector.tensor_scalar(u[:, t, :], x2[:, t, :], b_mv[:, t, 0:1], b_r1[:, t:t + 1],
                                                    ALU.subtract, ALU.mult)
                    if k == AT["n"]:
                        dve.wait_ge(s["b_mv"], 1)
                        dve.wait_ge(s["b_r12"], 1)
                        normalise(nn, x2, b_mv, b_r12, s["n_ready"])
                    if k == AT["dtx"]:
                        ps = wait_full(dve, "dt")
                        nc.vector.tensor_tensor(dtx[:], ps[:, 0:NT * MHEADS], dt_bias[:], ALU.add).then_inc(free("dt"), 1)
                    for n, at in enumerate(AT["conv"]):
                        if at == k:
                            convolve(*CONV_ORDER[n])
                    if k in AT["silu"]:
                        c = AT["silu"].index(k)
                        dve.wait_ge(s["tanh_ready"], c + 1)
                        nc.vector.scalar_tensor_tensor(out=xbc[:, c, :], in0=xbc[:, c, :], scalar=1.0, in1=acc[c],
                                                       op0=ALU.add, op1=ALU.mult).then_inc(s["silu_ready"], 1)
                    if k in AT["zsilu"]:
                        c = AT["zsilu"].index(k)
                        dve.wait_ge(s["ztanh_ready"], c + 1)
                        ps = wait_full(dve, f"z{c}")
                        nc.vector.scalar_tensor_tensor(out=zs[:, c, :], in0=zs[:, c, :], scalar=1.0, in1=ps[:],
                                                       op0=ALU.add, op1=ALU.mult).then_inc(free(f"z{c}"), 1)
                    if k in AT["xdt"]:
                        n = AT["xdt"].index(k)
                        dve.wait_ge(s["dt_ready"], 1)
                        ps = wait_full(dve, f"xdt{n}")
                        nc.vector.tensor_tensor(
                            xdt[:, 2 * n:2 * n + 2, :].rearrange("p t (h d) -> p (t h) d", d=HD),
                            ps[:].rearrange("p (g d) -> p g d", d=HD),
                            dt[:, 8 * n:8 * n + 8].unsqueeze(2).to_broadcast([P, 8, HD]),
                            ALU.mult).then_inc(free(f"xdt{n}"), 1)
                    if k in AT["scan"]:
                        h, part = divmod(AT["scan"].index(k), 2)
                        scan(h, (1, 2, 3) if part else (0,))
                    if k in AT["y"]:
                        c = AT["y"].index(k)
                        ps = wait_full(dve, f"y{c}")
                        dve.wait_ge(s["silu_ready"], c + 1)
                        nc.vector.scalar_tensor_tensor(out=yd[:, c, :], in0=xbc[:, c, :], scalar=d_col[:, c:c + 1],
                                                       in1=ps[:], op0=ALU.mult, op1=ALU.add).then_inc(free(f"y{c}"), 1)
                        wait_read(dve, f"y{c}")
                        wait_read(dve, f"z{c}")
                        nc.vector.tensor_tensor(yz[:, c, :], yd[:, c, :], zs[:, c, :], ALU.mult).then_inc(s["yz_ready"], 1)
                    if k == AT["ss"]:
                        ps = wait_full(dve, "ss")
                        nc.vector.tensor_scalar(ss[:], ps[:, 0:NT], 1.0 / INNER, LN_EPS, ALU.mult,
                                                ALU.add).then_inc(free("ss"), 1)
                    if k == AT["u2"]:
                        dve.wait_ge(s["rs_ready"], 1)
                        ps = wait_full(dve, "mo")
                        for t in range(NT):
                            last = nc.vector.scalar_tensor_tensor(
                                out=u2[:, t, :], in0=ps[:, P * t:P * t + P], scalar=rs[:, t:t + 1], in1=u[:, t, :],
                                op0=ALU.mult, op1=ALU.add)
                        last.then_inc(free("mo"), 1)
                    if k == AT["h3"]:
                        wait_read(dve, "mo")
                        dve.wait_ge(s["r3_ready"], 1)
                        for t in range(NT):
                            nc.vector.tensor_scalar(h3[:, t, :], u2[:, t, :], r3[:, t:t + 1], None,
                                                    ALU.mult).then_inc(s["h3_ready"], 1)
                    if k == AT["x3"]:
                        add_to(x3, "mlp", x2b, s["x2b_ready"], 1)
                        statistics(x3, st4, d_mv, s["d_mv"])
                    if k == AT["norm4"]:
                        dve.wait_ge(s["d_mv"], 1)
                        dve.wait_ge(s["d_rstd"], 1)
                        normalise(n4, x3, d_mv, d_rstd, s["n4_ready"])
                    if k == AT["x4"]:
                        add_to(x4, "ffn2", x3b, s["x3b_ready"], NT)

                def front_part(k):
                    if k == AT["front_stats"]:
                        dve.wait_ge(s["x_loaded"], 16)
                        statistics(xin, x_st, x_mv, s["x_mv"])
                    if k == AT["front_norm"]:
                        dve.wait_ge(s["x_mv"], 1)
                        dve.wait_ge(s["x_rstd"], 1)
                        normalise(xn, xin, x_mv, x_rstd, s["xn_ready"])
                    if k == AT["front_split"]:
                        if setup:
                            low_m(0)
                        wait_read(dve, "nxT")
                        if att:
                            dve.wait_ge(s["s_full"], USES * HEADS)
                        nc.vector.tensor_copy(hTh[:], hT).then_inc(s["hTh_ready"], 1)
                        dve.wait_ge(s["hTh_ready"], 1)
                        nc.vector.tensor_tensor(hTl[:], hT, hTh[:].bitcast(F32), ALU.subtract).then_inc(s["hTl_ready"], 1)
                    if k == AT["front_gh"]:
                        wait_read(dve, "gx")
                        nc.vector.tensor_copy(Gh[0][:], G[:]).then_inc(s["front_gh"], 1)
                        if setup:
                            for n in (1, 2, 3):
                                low_m(n)
                            dve.wait_ge(su_pe, 6)
                            nc.vector.tensor_tensor(row_out_b[:], psO[:, 0:P], row_out_b[:], ALU.add)

                def fold_part(k):
                    if "lora3" in FOLD_AT.get(k, []):
                        dve.wait_ge(tail_loaded, TAIL_LOADED)
                        ps = wait_full(dve, "lora3")
                        nc.vector.tensor_tensor(ffn_wt[:], ps[:, 0:P], ffn_wt[:], ALU.add).then_inc(free("lora3"), 1)
                        nc.vector.tensor_scalar(win_t[:, INNER:], win_t[:, INNER:], norm1[:, 0:1], None, ALU.mult)
                        nc.vector.tensor_scalar(win_t[:, 0:INNER], win_t[:, 0:INNER], norm1[:, 0:1], 0.5, ALU.mult, ALU.mult)
                        nc.vector.tensor_scalar(conv_w[:], conv_w[:], 0.5, None, ALU.mult)
                        nc.vector.tensor_scalar(conv_b[:], conv_b[:], 0.5, None, ALU.mult)
                        nc.vector.tensor_scalar(w1[:], w1[:], norm2[:, 0:1], None, ALU.mult)
                        for k in range(2):
                            nc.vector.tensor_scalar(wmo[:, k, :], wmo[:, k, :], mnorm[:, k:k + 1], None, ALU.mult)

                for k in range(SLOTS):
                    step, t = divmod(k, NT)
                    if fold:
                        fold_part(k)
                    if att:
                        for p in pairs_at(k, "invert"):
                            invert(p)
                        if step < HEADS:
                            mask_and_max(step, t)
                        if 0 <= k - V_AT - V_LATER < 2 * NT and (k - V_AT - V_LATER) % 2 == 1:
                            copy_v(k - V_AT - V_LATER)
                        if t >= ACT_TILES and 1 <= step <= HEADS:
                            copy_t(step - 1, t)
                        if t == G_AT["split"] and step + 1 < HEADS:
                            split_g(step + 1)
                        for p in pairs_at(k, "normalise"):
                            normalise_o(p)
                    if tail:
                        tail_part(k)
                    if front:
                        front_part(k)
                if att:
                    end()

            @block.gpsimd
            def _(pool):
                chained = [0]

                def chain(last):
                    chained[0] += 1
                    last.then_inc(s["pool_chain"], 1)
                    pool.wait_ge(s["pool_chain"], chained[0])

                def inverse_deviation(mv, veps, rstd, mv_ready, ready):
                    pool.wait_ge(mv_ready, 1)
                    chain(nc.gpsimd.tensor_scalar(veps[:], mv[:, :, 1], LN_EPS, None, ALU.add))
                    nc.gpsimd.tensor_tensor(rstd[:], veps[:], neg_half[:], ALU.pow).then_inc(ready, 1)

                def add_rows(dst, x, row, ready):
                    for t in range(NT):
                        nc.gpsimd.tensor_tensor(dst[:, t, :], x[:, t, :], row[:], ALU.add).then_inc(ready, 1)

                def split_g(h):
                    pool.wait_ge(s["gh_ready"], h)
                    if h >= 2:
                        pool.wait_ge(s["s_full"], USES * (h - 1))
                    nc.gpsimd.tensor_tensor(Gl[h % 2][:], G[:], Gh[h % 2][:].bitcast(F32),
                                            ALU.subtract).then_inc(s["gl_ready"], 1)

                def spread(p):
                    pool.wait_ge(s["rden_ready"], p + 1)
                    if p >= 1:
                        pool.wait_ge(s["o_ready"], p)
                    for t in range(NT):
                        last = nc.gpsimd.tensor_copy(R[:, P * t:P * t + P].rearrange("p (h d) -> p h d", d=HD),
                                                     rden[:, 2 * p:2 * p + 2, t:t + 1].to_broadcast([P, 2, HD]))
                    last.then_inc(s["spread_ready"], 1)

                def tail_part(k):
                    if k == AT["rstd1"]:
                        inverse_deviation(a_mv, a_veps, a_rstd, s["a_mv"], s["a_rstd"])
                        add_rows(x1b, x1, ffn_b, s["x1b_ready"])
                    if k == AT["r12"]:
                        pool.wait_ge(s["b_mv"], 1)
                        chain(nc.gpsimd.tensor_scalar(b_veps[:], b_mv[:, :, 1], LN_EPS, None, ALU.add))
                        chain(nc.gpsimd.tensor_tensor(b_r1[:], b_veps[:], neg_half[:], ALU.pow))
                        chain(nc.gpsimd.tensor_tensor(b_sq[:], b_r1[:], b_r1[:], ALU.mult))
                        chain(nc.gpsimd.tensor_tensor(b_sq[:], b_sq[:], b_mv[:, :, 1], ALU.mult))
                        chain(nc.gpsimd.tensor_scalar(b_sq[:], b_sq[:], float(P), BN_EPS, ALU.mult, ALU.add))
                        chain(nc.gpsimd.tensor_tensor(b_r2[:], b_sq[:], neg_half[:], ALU.pow))
                        nc.gpsimd.tensor_tensor(b_r12[:], b_r1[:], b_r2[:], ALU.mult).then_inc(s["b_r12"], 1)
                    if k == AT["softplus"]:
                        wait_read(pool, "dt")
                        chain(nc.gpsimd.tensor_scalar(dt_s[:], dtx[:], 0.0, 2.0, ALU.max, ALU.mult))
                        nc.gpsimd.tensor_tensor(dt_abs[:], dt_s[:], dtx[:], ALU.subtract).then_inc(s["dt_abs"], 1)
                    if k == AT["softplus_end"]:
                        pool.wait_ge(s["dt_exp"], 1)
                        chain(nc.gpsimd.tensor_scalar(dt_s[:], dt_exp[:], 2.0, None, ALU.add))
                        chain(nc.gpsimd.tensor_tensor(dt_s2[:], dt_s[:], neg_one[:], ALU.pow))
                        chain(nc.gpsimd.tensor_tensor(dt_s[:], dt_exp[:], dt_s2[:], ALU.mult))
                        chain(nc.gpsimd.tensor_tensor(dt_s2[:], dt_s[:], dt_s[:], ALU.mult))
                        coef = [2.0 / (2 * k + 1) for k in range(LOG_TERMS)]
                        chain(nc.gpsimd.tensor_scalar(dt_poly[:], dt_s2[:], coef[-1], coef[-2], ALU.mult, ALU.add))
                        for c in coef[LOG_TERMS - 3::-1]:
                            chain(nc.gpsimd.tensor_tensor(dt_poly[:], dt_poly[:], dt_s2[:], ALU.mult))
                            chain(nc.gpsimd.tensor_scalar(dt_poly[:], dt_poly[:], c, None, ALU.add))
                        chain(nc.gpsimd.tensor_tensor(dt_poly[:], dt_poly[:], dt_s[:], ALU.mult))
                        chain(nc.gpsimd.tensor_scalar(dt_s[:], dtx[:], 0.0, None, ALU.max))
                        nc.gpsimd.tensor_tensor(dt[:], dt_s[:], dt_poly[:], ALU.add).then_inc(s["dt_ready"], 1)
                        pool.wait_ge(s["dt_ready"], 1)
                        nc.gpsimd.tensor_tensor(dta[:], dt[:], exp_a[:], ALU.mult).then_inc(s["dta_ready"], 1)
                    if k in AT["mul"]:
                        h, part = divmod(AT["mul"].index(k), 2)
                        if part == 0:
                            for n in range(len(BC_TILES)):
                                wait_read(pool, f"bc{n}")
                            wait_read(pool, f"da{h}")
                            if h >= 2:
                                pool.wait_ge(full("y0"), count("y0"))
                        cols = slice(TRI // 2 * part, TRI // 2 * (part + 1))
                        nc.gpsimd.tensor_tensor(M[h % 2][:, cols], L[h % 2][:, cols], bc[:, cols],
                                                ALU.mult).then_inc(s["m_ready"], 1)
                    if k == AT["rs"]:
                        wait_read(pool, "ss")
                        nc.gpsimd.tensor_tensor(rs[:], ss[:], neg_half[:], ALU.pow).then_inc(s["rs_ready"], 1)
                    if k == AT["r3"]:
                        pool.wait_ge(s["ss2_ready"], NT)
                        chain(nc.gpsimd.tensor_scalar(r3_eps[:], ss2[:], BN_EPS, None, ALU.add))
                        nc.gpsimd.tensor_tensor(r3[:], r3_eps[:], neg_half[:], ALU.pow).then_inc(s["r3_ready"], 1)
                    if k == AT["x2b"]:
                        wait_read(pool, "mo")
                        for t in range(NT):
                            last = nc.gpsimd.tensor_tensor(x2b[:, t, :], x2[:, t, :], u2[:, t, :], ALU.add)
                        chain(last)
                        for t in range(NT):
                            last = nc.gpsimd.tensor_tensor(x2b[:, t, :], x2b[:, t, :], b2[:], ALU.add)
                        last.then_inc(s["x2b_ready"], 1)
                    if k == AT["rstd4"]:
                        inverse_deviation(d_mv, d_veps, d_rstd, s["d_mv"], s["d_rstd"])
                    if k == AT["x3b"]:
                        pool.wait_ge(s["d_mv"], 1)
                        add_rows(x3b, x3, ffn_b, s["x3b_ready"])

                def front_part(k):
                    if k == AT["front_rstd"]:
                        inverse_deviation(x_mv, x_veps, x_rstd, s["x_mv"], s["x_rstd"])
                    if k == AT["front_gl"]:
                        pool.wait_ge(s["front_gh"], 1)
                        nc.gpsimd.tensor_tensor(Gl[0][:], G[:], Gh[0][:].bitcast(F32), ALU.subtract).then_inc(s["front_gl"], 1)
                        pool.wait_ge(s["front_gl"], 1)
                        if setup:
                            pool.wait_ge(su_act, 6)
                            nc.gpsimd.tensor_tensor(wvl[:], wv, wvh[:].bitcast(F32), ALU.subtract).then_inc(su_pool, 1)
                            pool.wait_ge(su_pool, 2)

                if setup:
                    nc.gpsimd.memset(neg_half[:], -0.5)
                    nc.gpsimd.memset(neg_one[:], -1.0)
                    nc.gpsimd.memset(ones[:], 1.0)
                    nc.gpsimd.memset(pad[:], 0.0).then_inc(su_pool, 1)
                    pool.wait_ge(su_pool, 1)
                if att:
                    add_rows(xb, xin, row_out_b, s["xb_ready"])
                for k in range(SLOTS):
                    step, t = divmod(k, NT)
                    if att:
                        if t == G_AT["rest"] and step + 1 < HEADS:
                            split_g(step + 1)
                        for p in pairs_at(k, "spread"):
                            spread(p)
                    if tail:
                        tail_part(k)
                    if front:
                        front_part(k)

        batch = a["x"].shape[0]
        with nc.Block() as block:
            iteration(None, None, 0, block)
        nc.all_engine_barrier(sems_to_clear=loop_sems)
        with nc.Block() as block:
            iteration(0, None, 1, block)
        nc.all_engine_barrier(sems_to_clear=loop_sems)
        with nc.Fori(1, batch) as i:
            with nc.Block() as block:
                iteration(i, i - 1, (i + 1) % batch, block)
            nc.all_engine_barrier(sems_to_clear=loop_sems)
        with nc.Block() as block:
            iteration(None, batch - 1, None, block)


def kernel(**inputs):
    import concourse.bacc as bacc
    from concourse.bass_utils import run_bass_kernel_spmd

    g = {k: np.asarray(v) for k, v in inputs.items()}
    w = g["L0_attn_a_qkv_w"].transpose(1, 2, 0)

    def pairs(m):
        return m.reshape(PAIRS, P, -1).transpose(1, 0, 2)

    def columns(v):
        return v.reshape(-1, P).T

    def rows(v, times=1):
        return np.tile(v.reshape(1, -1), (P, times))

    eye = np.eye(P, dtype=np.float32)
    causal = np.zeros((P, TOK), np.float32)
    causal[:, TOK - P:] = np.triu(np.full((P, P), MASKED, np.float32), 1)
    eye_row = np.zeros((P, TOK), np.float32)
    eye_row[:, :P] = eye
    bq = np.zeros((2, HD, PAIRS, 2), np.float32)
    for half in range(2):
        bq[half, :, :, half] = g["L0_attn_a_qkv_b"][half::2, 0:HD].T
    bq = bq.reshape(P, PAIRS, 2)
    arrays = {
        "x": g["L0_attn_a_x"],
        "wq_t": pairs(w[:, 0:HD]), "wk_t": pairs(w[:, HD:2 * HD]),
        "wv": g["L0_attn_a_qkv_w"][:, :, 2 * HD:].reshape(P, HEADS * HD),
        "wo": pairs(g["L0_attn_a_out_w"]),
        "bq": bq, "bv": columns(g["L0_attn_a_qkv_b"][:, 2 * HD:]),
        "out_b": rows(g["L0_attn_a_out_b"]),
        "ffn_wt": g["L0_ffn_W"].T, "ffn_b": rows(g["L0_ffn_b"]), "up_t": g["L0_ffn_up_aux"].T,
        "lora_up_t": g["L0_ffn_lora_up"].T, "lora_down_t": g["L0_ffn_lora_down"].T,
        "down_aux": g["L0_ffn_down_aux"],
        "norm1": g["L0_attn_b_norm1_w"].reshape(P, 1), "norm2": g["L0_attn_b_norm2_w"].reshape(P, 1),
        "win_t": g["L0_attn_b_in_proj_w"].T,
        "conv_w": g["L0_attn_b_conv_w"].reshape(4, P, CONV).transpose(1, 0, 2),
        "conv_b": columns(g["L0_attn_b_conv_b"]),
        "dt_bias": rows(g["L0_attn_b_dt_bias"], NT), "a_log": rows(g["L0_attn_b_A_log"], NT),
        "d_col": columns(np.repeat(g["L0_attn_b_D"], HD)), "mnorm": columns(g["L0_attn_b_mnorm_w"]),
        "wmo": g["L0_attn_b_out_proj_w"].T.reshape(2, P, P).transpose(1, 0, 2),
        "w1": g["L0_attn_b_mlp_w1"].T, "b1": columns(g["L0_attn_b_mlp_b1"]),
        "w2": g["L0_attn_b_mlp_w2"].T.reshape(4, P, P).transpose(1, 0, 2), "b2": rows(g["L0_attn_b_mlp_b2"]),
        "mask": causal, "eye_row": eye_row,
    }
    nc = bacc.Bacc("TRN2", target_bir_lowering=False, num_devices=1)
    aps, ins = {}, {}
    for name, arr in arrays.items():
        arr = np.ascontiguousarray(arr)
        ins[f"in_{name}"] = arr
        aps[name] = nc.dram_tensor(f"in_{name}", arr.shape, mybir.dt.from_np(arr.dtype), kind="ExternalInput").ap()
    out = nc.dram_tensor("out", arrays["x"].shape, F32, kind="ExternalOutput").ap()
    layer(nc, aps, out)
    r = run_bass_kernel_spmd(nc, [ins], core_ids=[0])
    return r.results[0]["out"]
```
